# Optimizing a Trainium2 kernel written in Bass

```python
import numpy as np
import jax
import jax.numpy as jnp

def _softmax(x, axis=-1):
    return jax.nn.softmax(x, axis=axis)

def _gelu(x):
    return jax.nn.gelu(x, approximate=True)

def _silu(x):
    return jax.nn.silu(x)

def _sigmoid(x):
    return jax.nn.sigmoid(x)

def _layernorm(x, axis=-1, eps=1e-05):
    m = jnp.mean(x, axis=axis, keepdims=True)
    v = jnp.var(x, axis=axis, keepdims=True)
    return (x - m) / jnp.sqrt(v + eps)

def _scatter_add(tgt, idx, src, axis=0):
    return tgt.at[idx].add(src)

def _segment_sum(src, seg, n):
    return jax.ops.segment_sum(src, seg, n)
kernel_name = 'mk_seq_postln_d1_jaxref_r4_5f8911'

def setup_inputs(seed: int=0):
    np.random.seed(seed)
    _w = jnp.asarray

    def _L0_attn_setup():
        import jax, jax.numpy as jnp
        import numpy as np
        D_MODEL = 256
        N_HEADS = 16
        D_LATENT = 64
        HEAD_DIM = D_MODEL // N_HEADS

        def apply_rope(x):
            B, T, H, D = x.shape
            inv_freq = 1.0 / 10000.0 ** (jnp.arange(0, D, 2, dtype=jnp.float32) / D)
            t = jnp.arange(T, dtype=jnp.float32)
            freqs = t[:, None] * inv_freq[None, :]
            sin_f = jnp.sin(freqs)[None, :, None, :]
            cos_f = jnp.cos(freqs)[None, :, None, :]
            x1, x2 = jnp.split(x, 2, axis=-1)
            return jnp.concatenate([x1 * cos_f - x2 * sin_f, x1 * sin_f + x2 * cos_f], axis=-1)
        key = jax.random.key(seed)
        ks = jax.random.split(key, 10)
        B, T = (4, 1024)
        s = lambda fan_in: 1.0 / np.sqrt(fan_in)
        return {'x': jax.random.normal(ks[0], (B, T, D_MODEL), dtype=jnp.float32), 'Wq': jax.random.normal(ks[1], (D_MODEL, D_MODEL), dtype=jnp.float32) * s(D_MODEL), 'bq': jnp.zeros((D_MODEL,), jnp.float32), 'Wdown': jax.random.normal(ks[2], (D_MODEL, D_LATENT), dtype=jnp.float32) * s(D_MODEL), 'bdown': jnp.zeros((D_LATENT,), jnp.float32), 'Wup': jax.random.normal(ks[3], (D_LATENT, 2 * D_MODEL), dtype=jnp.float32) * s(D_LATENT), 'bup': jnp.zeros((2 * D_MODEL,), jnp.float32), 'Wout': jax.random.normal(ks[4], (D_MODEL, D_MODEL), dtype=jnp.float32) * s(D_MODEL), 'bout': jnp.zeros((D_MODEL,), jnp.float32)}
    _L0_attn_in = _L0_attn_setup()

    def _L0_ffn_setup():
        import jax, jax.numpy as jnp
        import numpy as np
        TOP_K = 2
        EPS = 1e-09
        key = jax.random.key(seed)
        ks = jax.random.split(key, 6)
        B, T, D, H, E = (4, 512, 256, 512, 8)
        x = jax.random.normal(ks[0], (B, T, D), dtype=jnp.float32)
        Wg = jax.random.normal(ks[1], (E, D), dtype=jnp.float32) * 0.02
        W1 = jax.random.normal(ks[2], (E, 2 * H, D), dtype=jnp.float32) * 0.02
        b1 = jax.random.normal(ks[3], (E, 2 * H), dtype=jnp.float32) * 0.02
        Wo = jax.random.normal(ks[4], (D, H), dtype=jnp.float32) * 0.02
        bo = jax.random.normal(ks[5], (D,), dtype=jnp.float32) * 0.02
        return {'x': x, 'Wg': Wg, 'W1': W1, 'b1': b1, 'Wo': Wo, 'bo': bo}
    _L0_ffn_in = _L0_ffn_setup()
    _d = {'L0_attn_x': _L0_attn_in['x'], 'L0_attn_Wq': _L0_attn_in['Wq'], 'L0_attn_bq': _L0_attn_in['bq'], 'L0_attn_Wdown': _L0_attn_in['Wdown'], 'L0_attn_bdown': _L0_attn_in['bdown'], 'L0_attn_Wup': _L0_attn_in['Wup'], 'L0_attn_bup': _L0_attn_in['bup'], 'L0_attn_Wout': _L0_attn_in['Wout'], 'L0_attn_bout': _L0_attn_in['bout'], 'L0_ffn_Wg': _L0_ffn_in['Wg'], 'L0_ffn_W1': _L0_ffn_in['W1'], 'L0_ffn_b1': _L0_ffn_in['b1'], 'L0_ffn_Wo': _L0_ffn_in['Wo'], 'L0_ffn_bo': _L0_ffn_in['bo']}
    _x0 = _d['L0_attn_x']
    _d['L0_attn_x'] = jax.random.normal(jax.random.fold_in(jax.random.key(seed), 1), (4, 1024, 256), dtype=_x0.dtype)
    del _x0
    return _d

def reference(L0_attn_x, L0_attn_Wq, L0_attn_bq, L0_attn_Wdown, L0_attn_bdown, L0_attn_Wup, L0_attn_bup, L0_attn_Wout, L0_attn_bout, L0_ffn_Wg, L0_ffn_W1, L0_ffn_b1, L0_ffn_Wo, L0_ffn_bo):

    def _L0_attn_ref(x, Wq, bq, Wdown, bdown, Wup, bup, Wout, bout):
        import jax, jax.numpy as jnp
        import numpy as np
        D_MODEL = 256
        N_HEADS = 16
        D_LATENT = 64
        HEAD_DIM = D_MODEL // N_HEADS

        def apply_rope(x):
            B, T, H, D = x.shape
            inv_freq = 1.0 / 10000.0 ** (jnp.arange(0, D, 2, dtype=jnp.float32) / D)
            t = jnp.arange(T, dtype=jnp.float32)
            freqs = t[:, None] * inv_freq[None, :]
            sin_f = jnp.sin(freqs)[None, :, None, :]
            cos_f = jnp.cos(freqs)[None, :, None, :]
            x1, x2 = jnp.split(x, 2, axis=-1)
            return jnp.concatenate([x1 * cos_f - x2 * sin_f, x1 * sin_f + x2 * cos_f], axis=-1)
        B, T, D = x.shape
        H, Dh = (N_HEADS, HEAD_DIM)
        q = x @ Wq + bq
        kv_latent = x @ Wdown + bdown
        kv = kv_latent @ Wup + bup
        q = q.reshape(B, T, H, Dh)
        kv = kv.reshape(B, T, H, 2 * Dh)
        k, v = jnp.split(kv, 2, axis=-1)
        q = apply_rope(q)
        k = apply_rope(k)
        att = jnp.einsum('bthd,btgd->bthg', q, k) / jnp.sqrt(jnp.float32(Dh))
        att = jax.nn.softmax(att, axis=-1)
        out = jnp.einsum('bthg,btgd->bthd', att, v)
        out = out.reshape(B, T, D)
        return out @ Wout + bout

    def _L0_ffn_ref(x, Wg, W1, b1, Wo, bo):
        import jax, jax.numpy as jnp
        import numpy as np
        TOP_K = 2
        EPS = 1e-09
        E = Wg.shape[0]
        gate_logits = jnp.einsum('btd,ed->bte', x, Wg)
        gate_scores = jax.nn.softmax(gate_logits, axis=-1)
        topk_val, topk_idx = jax.lax.top_k(gate_scores, TOP_K)
        topk_val = topk_val / (topk_val.sum(axis=-1, keepdims=True) + EPS)
        comb = (jax.nn.one_hot(topk_idx, E, dtype=x.dtype) * topk_val[..., None]).sum(axis=-2)
        out = jnp.zeros_like(x)
        for e in range(E):
            h = jnp.einsum('btd,hd->bth', x, W1[e]) + b1[e]
            a, b = jnp.split(h, 2, axis=-1)
            g = a * jax.nn.sigmoid(b)
            eo = jnp.einsum('bth,dh->btd', g, Wo) + bo
            out = out + eo * comb[..., e:e + 1]
        return out
    x = L0_attn_x
    x = _layernorm(x + _L0_attn_ref(x, L0_attn_Wq, L0_attn_bq, L0_attn_Wdown, L0_attn_bdown, L0_attn_Wup, L0_attn_bup, L0_attn_Wout, L0_attn_bout), axis=-1)
    x = _layernorm(x + _L0_ffn_ref(x, L0_ffn_Wg, L0_ffn_W1, L0_ffn_b1, L0_ffn_Wo, L0_ffn_bo), axis=-1)
    return x

_drawn_inputs = setup_inputs


def setup_inputs(seed=0):
    import zlib

    import numpy as np

    out = dict(_drawn_inputs(seed))
    spreads = {'L0_attn_bq': (0.0, 0.274),
     'L0_attn_bdown': (0.0, 0.1),
     'L0_attn_bup': (0.0, 0.1),
     'L0_attn_bout': (0.0, 0.1)}
    factors = {'L0_ffn_b1': 8.0, 'L0_ffn_bo': 2.713}
    for name, (base, spread) in spreads.items():
        noise = np.random.default_rng([zlib.crc32(name.encode()), seed]).standard_normal(out[name].shape)
        drawn = base * np.exp(spread * noise) if base else spread * noise
        out[name] = jnp.asarray(drawn.astype(out[name].dtype))
    for name, factor in factors.items():
        out[name] = (out[name] * factor).astype(out[name].dtype)
    return out
```

```python
from contextlib import ExitStack

import numpy as np

import concourse.bass as bass
from concourse import mybir

F32 = mybir.dt.float32
BF16 = mybir.dt.bfloat16
U32 = mybir.dt.uint32
I32 = mybir.dt.int32
ALU = mybir.AluOpType
ACT = mybir.ActivationFunctionType
AX = mybir.AxisListType

P = 128
N, D = 4096, 256
NC = D // P
H, DH = 16, 16
HG = H * H
LAT = 64
E, HID = 8, 512
TOPK = 2
T = N // P
GT = 4
NG = T // GT
U = 2 * GT
BR = 256
CAP = N + BR
NB = N * TOPK // BR + E - 1
ZROW = E * CAP
ROWS = ZROW + BR
LN_EPS, GATE_EPS = 1e-5, 1e-9
QUARTER = DH ** -0.5

DS = 7
HS = 10


def shape_constants():
    inv = (np.float32(1.0) / np.power(np.float32(10000.0), np.arange(0, DH, 2, dtype=np.float32) / np.float32(DH))).astype(np.float32)
    ang = np.arange(1024, dtype=np.float32)[:, None] * inv[None, :]
    cos, sin = np.cos(ang).astype(np.float32), np.sin(ang).astype(np.float32)
    rope = np.stack([np.concatenate([cos, cos], 1), np.concatenate([-sin, sin], 1)], 1)
    rope = rope.reshape(U, P, 2 * DH).transpose(1, 0, 2)
    return {
        "rope": np.ascontiguousarray(rope),
        "eye": np.eye(P, dtype=np.float32),
        "before": np.triu(np.ones((P, P), np.float32), 1),
        "ones": np.ones((P, P), np.float32),
        "iota8": np.ascontiguousarray(np.broadcast_to(np.arange(E, dtype=np.float32), (P, E))),
        "base8": np.ascontiguousarray(np.broadcast_to(np.arange(E, dtype=np.float32) * CAP, (P, E))),
        "iotab": np.ascontiguousarray(np.broadcast_to(np.arange(NB, dtype=np.float32), (P, NB))),
    }


def bc(ap, shape):
    return ap.broadcast_to(shape)


def postln_kernel(nc, d, out):
    with ExitStack() as ctx:
        def sb(name, shape, dt=F32):
            return ctx.enter_context(nc.sbuf_tensor(name, shape, dt))

        def psum(name, shape):
            return ctx.enter_context(nc.psum_tensor(name, shape, F32))

        def sem(name):
            return ctx.enter_context(nc.semaphore(name))

        routed_x = nc.dram_tensor("routed_x", (ROWS, D), F32, kind="Internal").ap()
        x1_dram = nc.dram_tensor("x1_dram", (T, P, D), F32, kind="Internal").ap()
        routed_y = nc.dram_tensor("routed_y", (NB * BR, D), F32, kind="Internal").ap()

        eye = sb("eye", [P, P])
        before = sb("before", [P, P])
        ones = sb("ones_sb", [P, P])
        iota8 = sb("iota8", [P, E])
        base8 = sb("base8", [P, E])
        rope = sb("rope", [P, U, 2 * DH])
        wq = sb("wq", [P, NC, D])
        wdown = sb("wdown", [P, NC, LAT])
        bdown = sb("bdown", [LAT, 1])
        wup = sb("wup", [LAT, 2 * D])
        qk_bias = sb("qk_bias", [P, 2 * D])
        v_bias = sb("v_bias", [P, D])
        wout = sb("wout", [P, NC, D])
        bout = sb("bout", [P, D])
        wg = sb("wg", [P, NC, E])
        w1_hi = sb("w1_hi", [P, E, NC * 2 * HID], BF16)
        w1_lo = sb("w1_lo", [P, E, NC * 2 * HID], BF16)
        comb = sb("comb", [P, T, TOPK])
        pos_x = sb("pos_x", [P, T, TOPK])
        choice = sb("choice", [P, T, TOPK])
        pos = sb("pos", [P, T, TOPK], U32)
        shift = sb("shift", [P, T * TOPK])
        run = sb("run", [P, E])

        stage1 = ctx.enter_context(ExitStack())

        def sb1(name, shape, dt=F32):
            return stage1.enter_context(nc.sbuf_tensor(name, shape, dt))

        w1_raw = sb1("w1_raw", [P, NC * 2 * HID])
        xt = sb1("xt", [P, GT, NC, P])
        xtok = sb1("xtok", [P, GT, D])
        x1 = sb1("x1", [P, U, D])
        lat = sb1("lat", [LAT, 2, P])
        qk = sb1("qk", [P, 2 * D])
        qk_cos = sb1("qk_cos", [P, 2 * D])
        qk_sin = sb1("qk_sin", [P, 2 * D])
        qkr = sb1("qkr", [P, 2, 2 * D])
        v = sb1("v", [P, GT, D])
        sprod = sb1("sprod", [P, 2, DH, HG])
        smax = sb1("smax", [P, H])
        sdiff = sb1("sdiff", [P, 2, HG])
        probs = sb1("probs", [P, 2, HG])
        zsum = sb1("zsum", [P, H])
        zinv = sb1("zinv", [P, H])
        vprod = sb1("vprod", [P, HG, H])
        osum = sb1("osum", [P, D])
        onorm = sb1("onorm", [P, 2, D])
        ot = sb1("ot", [P, NC, P])
        res = sb1("res", [P, 2, D])
        stats = sb1("stats", [P, 6])
        mv = sb1("mv", [P, 2, 2])
        veps = sb1("veps", [P, 2])
        mhalf = sb1("mhalf", [P, 1])
        rstd = sb1("rstd", [P, 2])
        x1t = sb1("x1t", [P, NC, P])
        gmax = sb1("gmax", [P, GT])
        gdiff = sb1("gdiff", [P, GT, E])
        gexp = sb1("gexp", [P, GT, E])
        gz = sb1("gz", [P, GT])
        gzinv = sb1("gzinv", [P, GT])
        score = sb1("score", [P, GT, E])
        top = sb1("top", [P, GT, 8])
        topi = sb1("topi", [P, GT, 8], U32)
        topf = sb1("topf", [P, GT, TOPK])
        vsum = sb1("vsum", [P, GT])
        vinv = sb1("vinv", [P, GT])
        onehot = sb1("onehot", [P, GT, TOPK, E])
        member = sb1("member", [P, GT, E])
        pos8 = sb1("pos8", [P, GT, E])
        pos_sel = sb1("pos_sel", [P, GT, TOPK, E])
        posf = sb1("posf", [P, GT, TOPK])
        posi = sb1("posi", [P, 2, GT, TOPK], U32)

        count = sb("count", [P, E])
        count_i = sb("count_i", [P, E], I32)
        blocks_i = sb("blocks_i", [P, E], I32)
        blocks = sb("blocks", [P, E])
        blocks_to = sb("blocks_to", [P, E])
        first_row = sb("first_row", [P, E])
        expert_raw = sb("expert_raw", [P, NB])
        expert = sb("expert", [P, NB])
        row = sb("row", [P, NB])
        unused = sb("unused", [P, NB])
        row_fix = sb("row_fix", [P, NB])
        iotab = sb("iotab", [P, NB])
        tab_expert = sb("tab_expert", [P, NB], I32)
        tab_row = sb("tab_row", [P, NB], I32)
        tab_end = sb("tab_end", [P, E], I32)
        zeros = sb("zeros", [P, BR // P, D])

        CH = HID // P
        b1 = sb("b1", [P, E, 2, CH])
        wo_raw = sb("wo_raw", [P, CH, D])
        wo_hi = sb("wo_hi", [P, CH, D], BF16)
        wo_lo = sb("wo_lo", [P, CH, D], BF16)
        xrow = sb("xrow", [P, 3, BR // P, D])
        xt_hi = sb("xt_hi", [P, 3, NC, BR], BF16)
        xt_lo = sb("xt_lo", [P, 3, NC, BR], BF16)

        pick = sb("pick", [P, GT, TOPK], U32)
        bo = sb("bo", [P, D])
        comb_sum = sb("comb_sum", [P, T])
        stats3 = sb("stats3", [P, GT, 6])
        mv3 = sb("mv3", [P, 2, GT, 2])
        veps3 = sb("veps3", [P, GT])
        mhalf3 = sb("mhalf3", [P, GT])
        eps3 = sb("eps3", [P, GT])
        rstd3 = sb("rstd3", [P, 2, GT])

        sprod_all = sprod[:].rearrange("p b d n -> p (b d n)")
        vprod_all = vprod[:].rearrange("p a g -> p (a g)")
        sig = sprod_all[:, 0:1024].rearrange("p (c n) -> p c n", c=CH)
        gated = sprod_all[:, 1024:2048].rearrange("p (c n) -> p c n", c=CH)
        g_hi = sprod_all[:, 2048:3584].bitcast(BF16).rearrange("p (b c n) -> p b c n", b=3, c=CH)
        g_lo = sprod_all[:, 3584:5120].bitcast(BF16).rearrange("p (b c n) -> p b c n", b=3, c=CH)
        yg = sprod_all[:, 5120:7168].rearrange("p (t s n) -> p t s n", t=GT, s=TOPK)
        yrow = w1_raw[:, 0:1536].rearrange("p (b r n) -> p b r n", b=3, r=BR // P)
        xr = xt[:].rearrange("p t c n -> p t (c n)")
        passed = vprod_all[:, 0:NB * E].rearrange("p (b e) -> p b e", e=E)
        is_expert = vprod_all[:, 512:512 + NB * E].rearrange("p (b e) -> p b e", e=E)
        of_expert = vprod_all[:, 1024:1024 + T * TOPK * E].rearrange("p (k e) -> p k e", e=E)
        res3 = vprod_all[:, 0:2048].rearrange("p (b t n) -> p b t n", b=2, t=GT)
        o3 = vprod_all[:, 2048:4096].rearrange("p (b t n) -> p b t n", b=2, t=GT)

        ps_qk = psum("ps_qk", [P, 512])
        ps_v = psum("ps_v", [P, 512])
        ps_s = psum("ps_s", [P, 512])
        ps_t = psum("ps_t", [P, 512])
        ps_x = psum("ps_x", [P, 512])
        ps_y = psum("ps_y", [P, 512])
        ps_g = psum("ps_g", [P, 512])
        ps_r = psum("ps_r", [P, 512])
        ps_lat = ps_t[0:LAT, D:D + P]
        logits = ps_g[:, 0:GT * E].rearrange("p (t e) -> p t e", e=E)
        ps_pos = ps_r[:, 0:GT * E].rearrange("p (t e) -> p t e", e=E)
        ps_tot = ps_r[:, GT * E:(GT + 1) * E]

        w_in = sem("w_in")
        x_in = [sem(f"x_in{k}") for k in range(GT)]
        xt_in = [sem(f"xt_in{k}") for k in range(GT)]
        w1_in = sem("w1_in")
        lat_ready, lat_copied = sem("lat_ready"), sem("lat_copied")
        qkv_ready, qkv_taken = sem("qkv_ready"), sem("qkv_taken")
        rope_step = sem("rope_step")
        sprod_dve, sprod_pool = sem("sprod_dve"), sem("sprod_pool")
        scores_ready, sm_step = sem("scores_ready"), sem("sm_step")
        exp_ready = sem("exp_ready")
        vprod_dve, vprod_pool = sem("vprod_dve"), sem("vprod_pool")
        norm_step = sem("norm_step")
        ot_ready, ot_copied = sem("ot_ready"), sem("ot_copied")
        y_ready, ln_step = sem("y_ready"), sem("ln_step")
        xb_ready, veps_ready, rstd_ready, x1_ready = sem("xb_ready"), sem("veps_ready"), sem("rstd_ready"), sem("x1_ready")
        x1t_ready, x1t_copied, x1_stored = sem("x1t_ready"), sem("x1t_copied"), sem("x1_stored")
        logits_ready, gexp_ready, route_step = sem("logits_ready"), sem("gexp_ready"), sem("route_step")
        count_ready = sem("count_ready")
        w1_hi_done, w1_lo_done = sem("w1_hi_done"), sem("w1_lo_done")
        const_set = sem("const_set")
        scattered, pos_kept = sem("scattered"), sem("pos_kept")
        stored = sem("stored")
        waits_met = sem("waits_met")
        w2_in = sem("w2_in")
        table_step, zeros_set, tails_zeroed = sem("table_step"), sem("zeros_set"), sem("tails_zeroed")
        wo_hi_done, wo_lo_done = sem("wo_hi_done"), sem("wo_lo_done")
        xrow_in = [sem(f"xrow_in{k}") for k in range(3)]
        xrow_t, xt_hi_done, xt_lo_done = sem("xrow_t"), sem("xt_hi_done"), sem("xt_lo_done")
        hidden_ready, sig_ready, g_step = sem("hidden_ready"), sem("sig_ready"), sem("g_step")
        yrow_ready, yrow_copied = sem("yrow_ready"), sem("yrow_copied")
        yrow_out = [sem(f"yrow_out{k}") for k in range(3)]
        picked = [sem(f"picked{k}") for k in range(GT)]
        gathered = [sem(f"gathered{k}") for k in range(GT)]
        xr_in = [sem(f"xr_in{k}") for k in range(GT)]
        comb_summed, mix_step, rstd3_step, out_ready = sem("comb_summed"), sem("mix_step"), sem("rstd3_step"), sem("out_ready")

        ROPE, SM, NORM, LN, ROUTE = 5, 2, 4, 3, 25
        WEIGHT_LOADS = 16
        LATE_LOADS = 4
        TABLE = 24
        GATED = 3 * CH
        MIX = 5 * GT
        hidden_bank = [ps_qk, ps_v, ps_s, ps_t]

        block = ctx.enter_context(nc.Block())

        def after_waits(eng):
            eng.sem_inc(waits_met, 1)

        def slots(eng, slot):
            for j in range(U):
                slot(0, j, False)
            with eng.Fori(1, T // U) as m:
                for j in range(U):
                    slot(m, j, True)
            for j in range(U):
                slot(T // U, j, False)

        def tile_of(m, j, lag, steady):
            lag += 2
            t = m * U + (j - lag)
            return t, (j - lag) % U, steady or 0 <= t < T, (lambda k: steady or t >= k)

        def rounds(m, j, lag):
            return m * 2 + (j - lag - 2) // GT + 1

        def group_of(m, j, steady):
            q = m * 2 + (j - 11) // GT
            return q, ((j - 11) // GT) % 2, j % GT == 3 and (steady or 0 <= q < NG), (lambda k: steady or q >= k)

        def block_slots(eng, slot):
            for m in range(2):
                for j in range(3):
                    slot(m, j, False)
            with eng.Fori(2, NB // 3) as m:
                for j in range(3):
                    slot(m, j, True)
            for j in range(3):
                slot(NB // 3, j, False)

        def block_of(m, j, lag, steady):
            t = m * 3 + (j - lag)
            return t, (j - lag) % 3, steady or 0 <= t < NB, (lambda k: steady or t >= k)

        def group_slots(eng, slot):
            for m in range(2):
                for j in range(2):
                    slot(m, j, False)
            with eng.Fori(2, NG // 2) as m:
                for j in range(2):
                    slot(m, j, True)
            slot(NG // 2, 0, False)

        def late_group(m, j, lag, steady):
            g = m * 2 + (j - lag)
            return g, (j - lag) % 2, steady or 0 <= g < NG, (lambda k: steady or g >= k)

        @block.sync
        def _(sp):
            sp.dma_start(xt[:, 0], d["xT"][0]).then_inc(xt_in[0], 16)
            for name, buf in (("wdown", wdown), ("bdown", bdown), ("wq", wq), ("wup", wup), ("qk_bias", qk_bias),
                              ("v_bias", v_bias), ("rope", rope), ("eye", eye), ("wout", wout), ("bout", bout),
                              ("wg", wg), ("before", before), ("ones", ones), ("iota8", iota8), ("base8", base8),
                              ("base8", run)):
                sp.dma_start(buf[:], d[name]).then_inc(w_in, 16)
            for t in range(1, GT):
                sp.dma_start(xt[:, t], d["xT"][t]).then_inc(xt_in[t], 16)

            def slot(m, j, steady):
                t, jt, live, past = tile_of(m, j, 0, steady)
                if live:
                    if past(GT):
                        sp.wait_ge(ln_step, LN * (t - GT) + 1)
                    sp.dma_start(xtok[:, jt % GT], d["x"][t]).then_inc(x_in[jt % GT], 16)
                t, jt, live, past = tile_of(m, j, -2, steady)
                if live and past(GT):
                    sp.wait_ge(qkv_ready, t - GT + 1)
                    sp.dma_start(xt[:, jt % GT], d["xT"][t]).then_inc(xt_in[jt % GT], 16)
                t, jt, live, past = tile_of(m, j, 4, steady)
                if live:
                    sp.wait_ge(x1_ready, t + 1)
                    sp.dma_start(x1_dram[t], x1[:, jt]).then_inc(x1_stored, 16)
                    sp.wait_ge(x1_stored, 16 * (t + 1))
                    after_waits(sp)
                if j % GT == 0 and (steady or m * 2 + j // GT < NG):
                    g = m * 2 + j // GT
                    if steady or g > 0:
                        sp.wait_ge(w1_hi_done, g)
                        sp.wait_ge(w1_lo_done, g)
                    sp.dma_start(w1_raw[:], d["w1"][g]).then_inc(w1_in, 16)

            sp.dma_start(b1[:], d["b1"]).then_inc(w2_in, 16)
            sp.dma_start(wo_raw[:], d["wo"]).then_inc(w2_in, 16)
            sp.dma_start(bo[:], d["bo"]).then_inc(w2_in, 16)
            sp.dma_start(iotab[:], d["iotab"]).then_inc(w2_in, 16)
            slots(sp, slot)
            sp.wait_ge(zeros_set, 1)
            sp.dma_start(routed_x[ZROW:ZROW + BR].rearrange("(r p) d -> p r d", p=P), zeros[:]).then_inc(tails_zeroed, 16)
            sp.wait_ge(scattered, 16 * T * TOPK)
            sp.wait_ge(table_step, TABLE)
            for e in range(E):
                end = sp.value_load(tab_end[0:1, e:e + 1], min_val=e * CAP, max_val=e * CAP + N)
                sp.dma_start(routed_x[bass.ds(end, BR)].rearrange("(r p) d -> p r d", p=P),
                             zeros[:]).then_inc(tails_zeroed, 16)
            sp.wait_ge(tails_zeroed, 16 * (E + 1))

            def block_slot(m, j, steady):
                b, jb, live, past = block_of(m, j, 0, steady)
                if live:
                    if past(3):
                        sp.wait_ge(xrow_t, b - 2)
                    src = sp.value_load(tab_row[0:1, bass.ds(b, 1)], min_val=0, max_val=ROWS - BR)
                    sp.dma_start(xrow[:, jb], routed_x[bass.ds(src, BR)].rearrange("(r p) d -> p r d", p=P)
                                 ).then_inc(xrow_in[jb], 16)
                b, jb, live, past = block_of(m, j, 3, steady)
                if live:
                    sp.wait_ge(yrow_copied, b + 1)
                    sp.dma_start(routed_y.rearrange("(b r p) d -> b p r d", p=P, r=BR // P)[b], yrow[:, jb]
                                 ).then_inc(yrow_out[jb], 16)

            block_slots(sp, block_slot)

            def group_slot(m, j, steady):
                g, k, live, past = late_group(m, j, 0, steady)
                if live:
                    for n in range(GT):
                        if past(1):
                            sp.wait_ge(mix_step, MIX * (g - 1) + 5 * n + 1)
                        sp.dma_start(xr[:, n], x1_dram[g * GT + n]).then_inc(xr_in[n], 16)
                g, k, live, past = late_group(m, j, 1, steady)
                if live:
                    sp.wait_ge(out_ready, g + 1)
                    sp.dma_start(out.rearrange("(g n p) d -> g p n d", p=P, n=GT)[g], o3[:, k]).then_inc(stored, 16)

            group_slots(sp, group_slot)
            sp.wait_ge(stored, 16 * NG)

        @block.tensor
        def _(pe):
            def latent(m, j, t, jt, past):
                pe.wait_ge(xt_in[jt % GT], 16 * rounds(m, j, -2))
                if past(1):
                    pe.wait_ge(lat_copied, t)
                if past(6):
                    pe.wait_ge(ot_copied, t - 5)
                for c in range(NC):
                    mm = pe.matmul(ps_lat, wdown[:, c], xt[:, jt % GT, c], start=(c == 0), stop=(c == NC - 1))
                mm.then_inc(lat_ready, 1)

            def qkv(t, jt, past):
                pe.wait_ge(lat_copied, t + 1)
                if past(1):
                    pe.wait_ge(qkv_taken, t)
                for c in range(NC):
                    pe.matmul(ps_qk[:, 0:D], xt[:, jt % GT, c], wq[:, c], start=(c == 0), stop=(c == NC - 1))
                pe.matmul(ps_qk[:, D:2 * D], lat[:, jt % 2], wup[:, 0:D], start=True, stop=True)
                pe.matmul(ps_v[:, 0:D], lat[:, jt % 2], wup[:, D:2 * D], start=True, stop=True).then_inc(qkv_ready, 1)

            pe.wait_ge(w_in, 16 * WEIGHT_LOADS)

            def slot(m, j, steady):
                t, jt, live, past = tile_of(m, j, 3, steady)
                if live:
                    pe.wait_ge(norm_step, NORM * (t + 1))
                    if past(1):
                        pe.wait_ge(ot_copied, t)
                    pe.wait_ge(lat_copied, t + 5 if steady else min(t + 5, T))
                    for c in range(NC):
                        tr = pe.transpose(ps_t[:, c * P:(c + 1) * P], onorm[:, jt % 2, c * P:(c + 1) * P], eye[:])
                    tr.then_inc(ot_ready, 1)
                t, jt, live, past = tile_of(m, j, -2, steady)
                if live:
                    latent(m, j, t, jt, past)
                t, jt, live, past = tile_of(m, j, 5, steady)
                if live:
                    pe.wait_ge(x1_ready, t + 1)
                    if past(1):
                        pe.wait_ge(x1t_copied, t)
                    for c in range(NC):
                        tr = pe.transpose(ps_x[:, c * P:(c + 1) * P], x1[:, jt, c * P:(c + 1) * P], eye[:])
                    tr.then_inc(x1t_ready, 1)
                t, jt, live, past = tile_of(m, j, 3, steady)
                if live:
                    pe.wait_ge(ot_copied, t + 1)
                    if past(1):
                        pe.wait_ge(ln_step, LN * (t - 1) + 1)
                    for c in range(NC):
                        mm = pe.matmul(ps_y[:, 0:D], ot[:, c], wout[:, c], start=(c == 0), stop=(c == NC - 1))
                    mm.then_inc(y_ready, 1)
                t, jt, live, past = tile_of(m, j, 1, steady)
                if live:
                    b = jt % 2
                    pe.wait_ge(sprod_dve, t + 1)
                    pe.wait_ge(sprod_pool, t + 1)
                    if past(1):
                        pe.wait_ge(sm_step, SM * t)
                    for k in range(DH):
                        mm = pe.matmul(ps_s[:, 0:HG], eye[:], sprod[:, b, k], start=(k == 0), stop=(k == DH - 1))
                    mm.then_inc(scores_ready, 1)
                t, jt, live, past = tile_of(m, j, -1, steady)
                if live:
                    qkv(t, jt, past)
                t, jt, live, past = tile_of(m, j, 5, steady)
                if live:
                    pe.wait_ge(x1t_copied, t + 1)
                    if jt % GT == 0 and past(GT):
                        pe.wait_ge(route_step, ROUTE * (rounds(m, j, 5) - 2) + 2)
                    for c in range(NC):
                        mm = pe.matmul(logits[:, jt % GT], x1t[:, c], wg[:, c], start=(c == 0), stop=(c == NC - 1))
                    mm.then_inc(logits_ready, 1)
                q, k, live, past = group_of(m, j, steady)
                if live:
                    pe.wait_ge(route_step, ROUTE * q + 19)
                    for k in range(GT):
                        for kk in range(k):
                            pe.matmul(ps_pos[:, k], ones[:], member[:, kk], start=(kk == 0), stop=False)
                        pe.matmul(ps_pos[:, k], before[:], member[:, k], start=(k == 0), stop=True)
                    for k in range(GT):
                        mm = pe.matmul(ps_tot, ones[:], member[:, k], start=(k == 0), stop=(k == GT - 1))
                    mm.then_inc(count_ready, 1)

            slots(pe, slot)
            pe.wait_ge(w1_hi_done, E)
            pe.wait_ge(w1_lo_done, E)
            pe.wait_ge(wo_hi_done, 1)
            pe.wait_ge(wo_lo_done, 1)
            pe.wait_ge(table_step, TABLE)
            pe.wait_ge(gexp_ready, NG)

            def block_slot(m, j, steady):
                b, jb, live, past = block_of(m, j, 2, steady)
                if live:
                    e = pe.value_load(tab_expert[0:1, bass.ds(b, 1)], min_val=0, max_val=E - 1)
                    pe.wait_ge(xt_lo_done, b + 1)
                    for c in range(CH):
                        if past(1):
                            pe.wait_ge(g_step, GATED * (b - 1) + 3 * c + 1)
                        for half in range(2):
                            n = 0
                            for w, x in ((w1_hi, xt_hi), (w1_hi, xt_lo), (w1_lo, xt_hi)):
                                for kc in range(NC):
                                    at = kc * 2 * HID + half * HID + c * P
                                    mm = pe.matmul(hidden_bank[c][:, half * BR:(half + 1) * BR],
                                                   w[:, bass.ds(e, 1), at:at + P].rearrange("p o n -> p (o n)"), x[:, jb, kc],
                                                   start=(n == 0), stop=(n == 5))
                                    n += 1
                        mm.then_inc(hidden_ready, 1)
                b, jb, live, past = block_of(m, j, 3, steady)
                if live:
                    if past(1):
                        pe.wait_ge(yrow_copied, b)
                    pe.wait_ge(g_step, GATED * (b + 1))
                    for r in range(BR // P):
                        n = 0
                        for c in range(CH):
                            for gg, w in ((g_hi, wo_hi), (g_lo, wo_hi), (g_hi, wo_lo)):
                                mm = pe.matmul(ps_y[:, r * D:(r + 1) * D], gg[:, jb, c, r * P:(r + 1) * P], w[:, c],
                                               start=(n == 0), stop=(n == 3 * CH - 1))
                                n += 1
                    mm.then_inc(yrow_ready, 1)
                b, jb, live, past = block_of(m, j, 1, steady)
                if live:
                    pe.wait_ge(xrow_in[jb], 16 * (m + (j - 1) // 3 + 1))
                    if past(1):
                        pe.wait_ge(xt_lo_done, b)
                    for r in range(BR // P):
                        for c in range(NC):
                            tr = pe.transpose(ps_x[:, c * BR + r * P:c * BR + (r + 1) * P],
                                              xrow[:, jb, r, c * P:(c + 1) * P], eye[:])
                    tr.then_inc(xrow_t, 1)

            block_slots(pe, block_slot)

        @block.scalar
        def _(act):
            act.wait_ge(w_in, 16 * WEIGHT_LOADS)

            def copy_latent(t, jt, past):
                act.wait_ge(lat_ready, t + 1)
                if past(2):
                    act.wait_ge(qkv_ready, t - 1)
                act.activation(lat[:, jt % 2], ps_lat, ACT.Identity, bias=bdown[:]).then_inc(lat_copied, 1)


            def slot(m, j, steady):
                t, jt, live, past = tile_of(m, j, 3, steady)
                if live:
                    act.wait_ge(ot_ready, t + 1)
                    act.wait_ge(lat_ready, t + 6 if steady else min(t + 6, T))
                    if past(1):
                        act.wait_ge(y_ready, t)
                    act.copy(ot[:].rearrange("p c k -> p (c k)"), ps_t[:, 0:D]).then_inc(ot_copied, 1)
                t, jt, live, past = tile_of(m, j, -2, steady)
                if live:
                    copy_latent(t, jt, past)
                t, jt, live, past = tile_of(m, j, 5, steady)
                if live:
                    act.wait_ge(x1t_ready, t + 1)
                    if past(1):
                        act.wait_ge(logits_ready, t)
                    act.copy(x1t[:].rearrange("p c k -> p (c k)"), ps_x[:, 0:D]).then_inc(x1t_copied, 1)
                q, k, live, past = group_of(m, j, steady)
                if live:
                    act.wait_ge(route_step, ROUTE * q + 2)
                    act.activation(gexp[:], gdiff[:], ACT.Exp).then_inc(gexp_ready, 1)
                if j % GT == 2 and (steady or m * 2 + j // GT < NG):
                    g = m * 2 + j // GT
                    act.wait_ge(w1_in, 16 * (g + 1))
                    act.copy(w1_hi[:, g], w1_raw[:]).then_inc(w1_hi_done, 1)
                t, jt, live, past = tile_of(m, j, 1, steady)
                if live:
                    act.wait_ge(sm_step, SM * (t + 1))
                    if past(2):
                        act.wait_ge(norm_step, NORM * (t - 1))
                        act.wait_ge(vprod_pool, t - 1)
                    act.activation(probs[:, jt % 2], sdiff[:, jt % 2], ACT.Exp, scale=QUARTER).then_inc(exp_ready, 1)

            slots(act, slot)
            act.wait_ge(w2_in, 16 * LATE_LOADS)
            act.copy(wo_hi[:], wo_raw[:]).then_inc(wo_hi_done, 1)
            act.wait_ge(table_step, TABLE)

            def block_slot(m, j, steady):
                b, jb, live, past = block_of(m, j, 2, steady)
                if live:
                    e = act.value_load(tab_expert[0:1, bass.ds(b, 1)], min_val=0, max_val=E - 1)
                    for c in range(CH):
                        act.wait_ge(hidden_ready, CH * b + c + 1)
                        if past(1):
                            act.wait_ge(g_step, GATED * (b - 1) + 3 * c + 1)
                        act.activation(sig[:, c], hidden_bank[c][:, BR:2 * BR], ACT.Sigmoid,
                                       bias=b1[:, bass.ds(e, 1), 1, c:c + 1].rearrange("p o n -> p (o n)")).then_inc(sig_ready, 1)
                b, jb, live, past = block_of(m, j, 3, steady)
                if live:
                    act.wait_ge(yrow_ready, b + 1)
                    if past(3):
                        act.wait_ge(yrow_out[jb], 16 * (m + (j - 3) // 3))
                    act.copy(yrow[:, jb].rearrange("p r n -> p (r n)"), ps_y[:]).then_inc(yrow_copied, 1)
                b, jb, live, past = block_of(m, j, 1, steady)
                if live:
                    act.wait_ge(xrow_t, b + 1)
                    if past(3):
                        act.wait_ge(hidden_ready, CH * (b - 2))
                    act.copy(xt_hi[:, jb].rearrange("p c n -> p (c n)"), ps_x[:]).then_inc(xt_hi_done, 1)

            block_slots(act, block_slot)

        @block.gpsimd
        def _(pool):
            pool.memset(mhalf[:], -0.5).then_inc(const_set, 1)
            pool.wait_ge(const_set, 1)
            pool.wait_ge(w_in, 16 * WEIGHT_LOADS)

            def slot(m, j, steady):
                t, jt, live, past = tile_of(m, j, 2, steady)
                if live:
                    b = jt % 2
                    pool.wait_ge(exp_ready, t + 1)
                    if past(1):
                        pool.wait_ge(norm_step, NORM * (t - 1) + 3)
                    n = H - HS
                    pool.tensor_tensor(
                        vprod[:, HS * DH:].rearrange("p (h d) g -> p h d g", h=n),
                        probs[:, b, HS * H:].rearrange("p (h o g) -> p h o g", h=n, o=1).broadcast_to([P, n, DH, H]),
                        v[:, jt % GT].rearrange("p (o g d) -> p o d g", o=1, g=H).broadcast_to([P, n, DH, H]),
                        ALU.mult).then_inc(vprod_pool, 1)
                t, jt, live, past = tile_of(m, j, 0, steady)
                if live:
                    b = jt % 2
                    pool.wait_ge(rope_step, ROPE * (t + 1))
                    if past(2):
                        pool.wait_ge(scores_ready, t - 1)
                    n = DH - DS
                    qr = qkr[:, b, 0:D].rearrange("p (h o d) -> p d h o", h=H, o=1)[:, DS:].broadcast_to([P, n, H, H])
                    kr = qkr[:, b, D:2 * D].rearrange("p (o g d) -> p d o g", o=1, g=H)[:, DS:].broadcast_to([P, n, H, H])
                    pool.tensor_tensor(sprod[:, b, DS:].rearrange("p d (h g) -> p d h g", h=H), qr, kr,
                                       ALU.mult).then_inc(sprod_pool, 1)
                q, k, routed, past = group_of(m, j, steady)
                if routed:
                    pool.wait_ge(route_step, ROUTE * (q + 1))
                    after_waits(pool)
                    for n in range(GT):
                        for s in range(TOPK):
                            pool.indirect_dma_start(
                                routed_x, bass.IndirectOffsetOnAxis(ap=posi[:, k, n, s:s + 1], axis=0),
                                x1[:, k * GT + n], None).then_inc(scattered, 16)
                t, jt, live, past = tile_of(m, j, 1, steady)
                if live:
                    pool.wait_ge(x_in[jt % GT], 16 * rounds(m, j, 1))
                    pool.tensor_tensor(xtok[:, jt % GT], xtok[:, jt % GT], bout[:], ALU.add).then_inc(xb_ready, 1)
                t, jt, live, past = tile_of(m, j, 3, steady)
                if live:
                    b = jt % 2
                    pool.wait_ge(ln_step, LN * (t + 1))
                    if past(2):
                        pool.wait_ge(x1_ready, t - 1)
                        pool.wait_ge(rstd_ready, t - 1)
                    after_waits(pool)
                    pool.tensor_scalar(veps[:, b:b + 1], mv[:, b, 1:2], LN_EPS, None, ALU.add).then_inc(veps_ready, 1)
                    pool.wait_ge(veps_ready, t + 1)
                    pool.tensor_tensor(rstd[:, b:b + 1], veps[:, b:b + 1], mhalf[:], ALU.pow).then_inc(rstd_ready, 1)
                if routed:
                    pool.wait_ge(scattered, 16 * GT * TOPK * (q + 1))
            slots(pool, slot)
            pool.memset(mhalf3[:], -0.5).then_inc(const_set, 1)
            pool.memset(eps3[:], LN_EPS).then_inc(const_set, 1)
            pool.wait_ge(const_set, 3)
            pool.wait_ge(table_step, TABLE)
            for k in range(3):
                pool.wait_ge(yrow_out[k], 16 * (NB // 3))

            def group_slot(m, j, steady):
                g, k, live, past = late_group(m, j, 0, steady)
                if live:
                    for n in range(GT):
                        if past(1):
                            pool.wait_ge(mix_step, MIX * (g - 1) + 5 * n + 2)
                            pool.wait_ge(gathered[n], 32 * g)
                        pool.tensor_copy(pick[:, n], pos[:, bass.ds(g * GT + n, 1)].rearrange("p o s -> p (o s)")).then_inc(picked[n], 1)
                        pool.wait_ge(picked[n], g + 1)
                        after_waits(pool)
                        for s in range(TOPK):
                            pool.indirect_dma_start(
                                yg[:, n, s], None, routed_y,
                                bass.IndirectOffsetOnAxis(ap=pick[:, n, s:s + 1], axis=0)).then_inc(gathered[n], 16)
                g, k, live, past = late_group(m, j, 1, steady)
                if live:
                    pool.wait_ge(mix_step, MIX * (g + 1))
                    if past(1):
                        pool.wait_ge(rstd3_step, 2 * g)
                    pool.tensor_tensor(veps3[:], mv3[:, k, :, 1], eps3[:], ALU.add).then_inc(rstd3_step, 1)
                    pool.wait_ge(rstd3_step, 2 * g + 1)
                    if past(2):
                        pool.wait_ge(out_ready, g - 1)
                    pool.tensor_tensor(rstd3[:, k], veps3[:], mhalf3[:], ALU.pow).then_inc(rstd3_step, 1)

            group_slots(pool, group_slot)

        @block.vector
        def _(dve):
            dve.memset(zeros[:], 0.0).then_inc(zeros_set, 1)
            dve.wait_ge(w_in, 16 * WEIGHT_LOADS)

            def slot(m, j, steady):
                def normalise():
                    t, jt, live, past = tile_of(m, j, 4, steady)
                    if not live:
                        return
                    b = jt % 2
                    dve.wait_ge(rstd_ready, t + 1)
                    dve.tensor_scalar(x1[:, jt], res[:, b], mv[:, b, 0:1], rstd[:, b:b + 1], ALU.subtract,
                                      ALU.mult).then_inc(x1_ready, 1)

                t, jt, live, past = tile_of(m, j, 0, steady)
                if live:
                    b = jt % 2
                    dve.wait_ge(qkv_ready, t + 1)
                    if past(1):
                        dve.wait_ge(rope_step, ROPE * t)
                    dve.tensor_tensor(qk[:], ps_qk[:], qk_bias[:], ALU.add).then_inc(rope_step, 1)
                    if past(GT):
                        dve.wait_ge(vprod_dve, t - GT + 1)
                        dve.wait_ge(vprod_pool, t - GT + 1)
                    dve.tensor_tensor(v[:, jt % GT], ps_v[:, 0:D], v_bias[:], ALU.add).then_inc(qkv_taken, 1)
                    dve.wait_ge(rope_step, ROPE * t + 1)
                    heads = 2 * H
                    dve.tensor_tensor(
                        qk_cos[:].rearrange("p (h d) -> p h d", h=heads), qk[:].rearrange("p (h d) -> p h d", h=heads),
                        rope[:, jt, 0:DH].rearrange("p (o d) -> p o d", o=1).broadcast_to([P, heads, DH]),
                        ALU.mult).then_inc(rope_step, 1)
                    for half in range(2):
                        a, z = half * DH // 2, (1 - half) * DH // 2
                        dve.tensor_tensor(
                            qk_sin[:].rearrange("p (h d) -> p h d", h=heads)[:, :, a:a + DH // 2],
                            qk[:].rearrange("p (h d) -> p h d", h=heads)[:, :, z:z + DH // 2],
                            rope[:, jt, DH + a:DH + a + DH // 2].rearrange("p (o d) -> p o d", o=1)
                            .broadcast_to([P, heads, DH // 2]), ALU.mult).then_inc(rope_step, 1)
                normalise()
                if live:
                    dve.wait_ge(rope_step, ROPE * t + 4)
                    if past(2):
                        dve.wait_ge(sprod_pool, t - 1)
                        dve.wait_ge(sprod_dve, t - 1)
                    dve.tensor_tensor(qkr[:, b], qk_cos[:], qk_sin[:], ALU.add).then_inc(rope_step, 1)

                t2, jt2, live2, past2 = tile_of(m, j, 2, steady)
                b2 = jt2 % 2
                if live2:
                    dve.wait_ge(exp_ready, t2 + 1)
                    if past2(1):
                        dve.wait_ge(norm_step, NORM * t2)
                    dve.tensor_reduce(zsum[:], probs[:, b2].rearrange("p (h g) -> p h g", h=H), AX.X,
                                      ALU.add).then_inc(norm_step, 1)
                if live:
                    dve.wait_ge(rope_step, ROPE * (t + 1))
                    if past(2):
                        dve.wait_ge(scores_ready, t - 1)
                    qr = qkr[:, b, 0:D].rearrange("p (h o d) -> p d h o", h=H, o=1)[:, 0:DS].broadcast_to([P, DS, H, H])
                    kr = qkr[:, b, D:2 * D].rearrange("p (o g d) -> p d o g", o=1, g=H)[:, 0:DS].broadcast_to([P, DS, H, H])
                    dve.tensor_tensor(sprod[:, b, 0:DS].rearrange("p d (h g) -> p d h g", h=H), qr, kr,
                                      ALU.mult).then_inc(sprod_dve, 1)
                q, k, routed, routed_past = group_of(m, j, steady)
                if routed:
                    route(q, k, routed_past)
                if live2:
                    dve.wait_ge(norm_step, NORM * t2 + 1)
                    dve.reciprocal(zinv[:], zsum[:]).then_inc(norm_step, 1)
                    dve.tensor_tensor(
                        vprod[:, 0:HS * DH].rearrange("p (h d) g -> p h d g", h=HS),
                        probs[:, b2, 0:HS * H].rearrange("p (h o g) -> p h o g", h=HS, o=1).broadcast_to([P, HS, DH, H]),
                        v[:, jt2 % GT].rearrange("p (o g d) -> p o d g", o=1, g=H).broadcast_to([P, HS, DH, H]),
                        ALU.mult).then_inc(vprod_dve, 1)

                t3, jt3, live3, past3 = tile_of(m, j, 3, steady)
                b3 = jt3 % 2
                if live3:
                    dve.wait_ge(y_ready, t3 + 1)
                    dve.wait_ge(xb_ready, t3 + 1)
                    if past3(2):
                        dve.wait_ge(x1_ready, t3 - 1)
                    if past3(1):
                        dve.wait_ge(ln_step, LN * t3)
                    dve.tensor_tensor(res[:, b3], ps_y[:, 0:D], xtok[:, jt3 % GT], ALU.add).then_inc(ln_step, 1)

                if live2:
                    dve.wait_ge(vprod_pool, t2 + 1)
                    dve.wait_ge(vprod_dve, t2 + 1)
                    dve.tensor_reduce(osum[:], vprod[:], AX.X, ALU.add).then_inc(norm_step, 1)
                if live3:
                    dve.wait_ge(ln_step, LN * t3 + 1)
                    dve.bn_stats(stats[:], res[:, b3]).then_inc(ln_step, 1)
                if live2:
                    dve.wait_ge(norm_step, NORM * t2 + 3)
                    if past2(2):
                        dve.wait_ge(ot_ready, t2 - 1)
                    dve.tensor_tensor(
                        onorm[:, b2].rearrange("p (h d) -> p h d", h=H), osum[:].rearrange("p (h d) -> p h d", h=H),
                        zinv[:].rearrange("p (h o) -> p h o", o=1).broadcast_to([P, H, DH]), ALU.mult).then_inc(norm_step, 1)
                if live3:
                    dve.wait_ge(ln_step, LN * t3 + 2)
                    if past3(2):
                        dve.wait_ge(veps_ready, t3 - 1)
                    after_waits(dve)
                    dve.bn_aggr(mv[:, b3], stats[:]).then_inc(ln_step, 1)

                t1, jt1, live1, past1 = tile_of(m, j, 1, steady)
                if live1:
                    b1 = jt1 % 2
                    dve.wait_ge(scores_ready, t1 + 1)
                    if past1(1):
                        dve.wait_ge(sm_step, SM * t1)
                    sc = ps_s[:, 0:HG].rearrange("p (h g) -> p h g", h=H)
                    dve.tensor_reduce(smax[:], sc, AX.X, ALU.max).then_inc(sm_step, 1)
                    dve.wait_ge(sm_step, SM * t1 + 1)
                    if past1(2):
                        dve.wait_ge(exp_ready, t1 - 1)
                    dve.tensor_tensor(sdiff[:, b1].rearrange("p (h g) -> p h g", h=H), sc,
                                      smax[:].rearrange("p (h o) -> p h o", o=1).broadcast_to([P, H, H]),
                                      ALU.subtract).then_inc(sm_step, 1)

                if j % GT == 2 and (steady or m * 2 + j // GT < NG):
                    g = m * 2 + j // GT
                    dve.wait_ge(w1_hi_done, g + 1)
                    dve.tensor_tensor(w1_lo[:, g], w1_raw[:], w1_hi[:, g], ALU.subtract).then_inc(w1_lo_done, 1)

            def route(q, k, past):
                at = ROUTE * q
                dve.wait_ge(logits_ready, GT * (q + 1))
                dve.tensor_reduce(gmax[:], logits[:], AX.X, ALU.max).then_inc(route_step, 1)
                dve.wait_ge(route_step, at + 1)
                dve.tensor_tensor(gdiff[:], logits[:], gmax[:].rearrange("p (t o) -> p t o", o=1).broadcast_to([P, GT, E]),
                                  ALU.subtract).then_inc(route_step, 1)
                dve.wait_ge(gexp_ready, q + 1)
                dve.tensor_reduce(gz[:], gexp[:], AX.X, ALU.add).then_inc(route_step, 1)
                dve.wait_ge(route_step, at + 3)
                dve.reciprocal(gzinv[:], gz[:]).then_inc(route_step, 1)
                dve.wait_ge(route_step, at + 4)
                dve.tensor_tensor(score[:], gexp[:], gzinv[:].rearrange("p (t o) -> p t o", o=1).broadcast_to([P, GT, E]),
                                  ALU.mult).then_inc(route_step, 1)
                dve.wait_ge(route_step, at + 5)
                after_waits(dve)
                for n in range(GT):
                    dve.max(top[:, n], score[:, n]).then_inc(route_step, 1)
                dve.wait_ge(route_step, at + 9)
                after_waits(dve)
                for n in range(GT):
                    dve.max_index(topi[:, n], top[:, n], score[:, n]).then_inc(route_step, 1)
                dve.wait_ge(route_step, at + 13)
                dve.tensor_copy(topf[:], topi[:, :, 0:TOPK]).then_inc(route_step, 1)
                dve.scalar_tensor_tensor(out=vsum[:], in0=top[:, :, 0], scalar=GATE_EPS, in1=top[:, :, 1],
                                         op0=ALU.add, op1=ALU.add).then_inc(route_step, 1)
                dve.wait_ge(route_step, at + 14)
                for s in range(TOPK):
                    dve.tensor_tensor(onehot[:, :, s], iota8[:].rearrange("p (o e) -> p o e", o=1).broadcast_to([P, GT, E]),
                                      topf[:, :, s:s + 1].broadcast_to([P, GT, E]), ALU.is_equal).then_inc(route_step, 1)
                dve.wait_ge(route_step, at + 15)
                dve.reciprocal(vinv[:], vsum[:]).then_inc(route_step, 1)
                dve.wait_ge(route_step, at + 17)
                dve.tensor_tensor(member[:], onehot[:, :, 0], onehot[:, :, 1], ALU.add).then_inc(route_step, 1)
                dve.wait_ge(route_step, at + 18)
                dve.tensor_tensor(comb[:, bass.ds(q * GT, GT)], top[:, :, 0:TOPK],
                                  vinv[:].rearrange("p (t o) -> p t o", o=1).broadcast_to([P, GT, TOPK]),
                                  ALU.mult).then_inc(route_step, 1)
                dve.wait_ge(count_ready, q + 1)
                run_b = run[:].rearrange("p (o e) -> p o e", o=1).broadcast_to([P, GT, E])
                dve.tensor_tensor(pos8[:], ps_pos, run_b, ALU.add).then_inc(route_step, 1)
                dve.wait_ge(route_step, at + 21)
                for s in range(TOPK):
                    ins = dve.tensor_tensor(pos_sel[:, :, s], onehot[:, :, s], pos8[:], ALU.mult)
                ins.then_inc(route_step, 1)
                dve.tensor_tensor(run[:], run[:], ps_tot, ALU.add).then_inc(route_step, 1)
                dve.wait_ge(route_step, at + 22)
                dve.tensor_reduce(posf[:], pos_sel[:], AX.X, ALU.add).then_inc(route_step, 1)
                dve.wait_ge(route_step, at + 24)
                dve.tensor_copy(posi[:, k], posf[:]).then_inc(route_step, 1)
                dve.tensor_copy(pos_x[:, bass.ds(q * GT, GT)], posf[:])
                dve.tensor_copy(choice[:, bass.ds(q * GT, GT)], topf[:]).then_inc(pos_kept, 1)

            slots(dve, slot)
            dve.wait_ge(w2_in, 16 * LATE_LOADS)
            dve.wait_ge(pos_kept, NG)
            step = 0

            def table(ins, then=True):
                nonlocal step
                step += 1
                ins.then_inc(table_step, 1)
                if then:
                    dve.wait_ge(table_step, step)

            def over_blocks(a):
                return a.rearrange("p (o e) -> p o e", o=1).broadcast_to([P, NB, E])

            def over_experts(a):
                return a.rearrange("p (b o) -> p b o", o=1).broadcast_to([P, NB, E])

            table(dve.tensor_tensor(count[:], run[:], base8[:], ALU.subtract))
            table(dve.tensor_scalar(count_i[:], count[:], float(BR - 1), None, ALU.add))
            table(dve.tensor_scalar(blocks_i[:], count_i[:], BR.bit_length() - 1, None, ALU.logical_shift_right))
            table(dve.tensor_copy(blocks[:], blocks_i[:]))
            table(dve.tensor_tensor_scan(blocks_to[:], ones[:, 0:E], blocks[:], 0.0, ALU.mult, ALU.add))
            table(dve.tensor_tensor(passed, over_experts(iotab[:]), over_blocks(blocks_to[:]), ALU.is_ge))
            table(dve.tensor_reduce(expert_raw[:], passed, AX.X, ALU.add))
            table(dve.tensor_scalar(expert[:], expert_raw[:], float(E - 1), None, ALU.min))
            table(dve.tensor_tensor(is_expert, over_blocks(iota8[:]), over_experts(expert[:]), ALU.is_equal))
            table(dve.tensor_tensor(first_row[:], blocks_to[:], blocks[:], ALU.subtract))
            table(dve.scalar_tensor_tensor(out=first_row[:], in0=first_row[:], scalar=-float(BR), in1=base8[:],
                                           op0=ALU.mult, op1=ALU.add))
            table(dve.tensor_tensor(passed, is_expert, over_blocks(first_row[:]), ALU.mult))
            table(dve.tensor_reduce(row[:], passed, AX.X, ALU.add))
            table(dve.scalar_tensor_tensor(out=row[:], in0=iotab[:], scalar=float(BR), in1=row[:], op0=ALU.mult, op1=ALU.add))
            table(dve.tensor_scalar(unused[:], expert_raw[:], float(E) - 0.5, None, ALU.is_ge))
            table(dve.tensor_scalar(row_fix[:], row[:], -1.0, float(ZROW), ALU.mult, ALU.add))
            table(dve.tensor_tensor(row_fix[:], row_fix[:], unused[:], ALU.mult))
            table(dve.tensor_tensor(tab_row[:], row[:], row_fix[:], ALU.add), then=False)
            table(dve.tensor_copy(tab_expert[:], expert[:]), then=False)
            table(dve.tensor_copy(tab_end[:], run[:]))
            choices = choice[:].rearrange("p t (s o) -> p (t s) o", o=1).broadcast_to([P, T * TOPK, E])
            table(dve.tensor_tensor(of_expert, iota8[:].rearrange("p (o e) -> p o e", o=1)
                                    .broadcast_to([P, T * TOPK, E]), choices, ALU.is_equal))
            table(dve.tensor_tensor(of_expert, of_expert, first_row[:].rearrange("p (o e) -> p o e", o=1)
                                    .broadcast_to([P, T * TOPK, E]), ALU.mult))
            table(dve.tensor_reduce(shift[:], of_expert, AX.X, ALU.add))
            table(dve.tensor_tensor(pos[:].rearrange("p t s -> p (t s)"), pos_x[:].rearrange("p t s -> p (t s)"),
                                    shift[:], ALU.subtract), then=False)
            assert step == TABLE
            dve.wait_ge(wo_hi_done, 1)
            dve.tensor_tensor(wo_lo[:], wo_raw[:], wo_hi[:], ALU.subtract).then_inc(wo_lo_done, 1)
            dve.tensor_tensor(comb_sum[:], comb[:, :, 0], comb[:, :, 1], ALU.add).then_inc(comb_summed, 1)

            def block_slot(m, j, steady):
                b, jb, live, past = block_of(m, j, 2, steady)
                if live:
                    e = dve.value_load(tab_expert[0:1, bass.ds(b, 1)], min_val=0, max_val=E - 1)
                    if past(3):
                        dve.wait_ge(yrow_ready, b - 2)
                    for c in range(CH):
                        dve.wait_ge(sig_ready, CH * b + c + 1)
                        if past(1):
                            dve.wait_ge(g_step, GATED * (b - 1) + 3 * (c + 1))
                        dve.scalar_tensor_tensor(
                            out=gated[:, c], in0=hidden_bank[c][:, 0:BR],
                            scalar=b1[:, bass.ds(e, 1), 0, c:c + 1].rearrange("p o n -> p (o n)"),
                            in1=sig[:, c], op0=ALU.add, op1=ALU.mult).then_inc(g_step, 1)
                        dve.wait_ge(g_step, GATED * b + 3 * c + 1)
                        dve.tensor_copy(g_hi[:, jb, c], gated[:, c]).then_inc(g_step, 1)
                        dve.wait_ge(g_step, GATED * b + 3 * c + 2)
                        dve.tensor_tensor(g_lo[:, jb, c], gated[:, c], g_hi[:, jb, c], ALU.subtract).then_inc(g_step, 1)
                b, jb, live, past = block_of(m, j, 1, steady)
                if live:
                    dve.wait_ge(xt_hi_done, b + 1)
                    if past(3):
                        dve.wait_ge(hidden_ready, CH * (b - 2))
                    dve.tensor_tensor(xt_lo[:, jb].rearrange("p c n -> p (c n)"), ps_x[:],
                                      xt_hi[:, jb].rearrange("p c n -> p (c n)"), ALU.subtract).then_inc(xt_lo_done, 1)

            block_slots(dve, block_slot)
            dve.wait_ge(comb_summed, 1)

            def group_slot(m, j, steady):
                g, k, live, past = late_group(m, j, 0, steady)
                if live:
                    for n in range(GT):
                        at = MIX * g + 5 * n
                        tile = g * GT + n
                        dve.wait_ge(xr_in[n], 16 * (g + 1))
                        dve.wait_ge(gathered[n], 32 * (g + 1))
                        if past(2):
                            dve.wait_ge(out_ready, g - 1)
                        r = res3[:, k, n]
                        dve.scalar_tensor_tensor(out=r, in0=yg[:, n, 0], scalar=comb[:, bass.ds(tile, 1), 0], in1=xr[:, n],
                                                 op0=ALU.mult, op1=ALU.add).then_inc(mix_step, 1)
                        dve.wait_ge(mix_step, at + 1)
                        dve.scalar_tensor_tensor(out=r, in0=yg[:, n, 1], scalar=comb[:, bass.ds(tile, 1), 1], in1=r,
                                                 op0=ALU.mult, op1=ALU.add).then_inc(mix_step, 1)
                        dve.wait_ge(mix_step, at + 2)
                        dve.scalar_tensor_tensor(out=r, in0=bo[:], scalar=comb_sum[:, bass.ds(tile, 1)], in1=r,
                                                 op0=ALU.mult, op1=ALU.add).then_inc(mix_step, 1)
                        dve.wait_ge(mix_step, at + 3)
                        dve.bn_stats(stats3[:, n], r).then_inc(mix_step, 1)
                        dve.wait_ge(mix_step, at + 4)
                        if past(2):
                            dve.wait_ge(rstd3_step, 2 * (g - 1))
                        after_waits(dve)
                        dve.bn_aggr(mv3[:, k, n], stats3[:, n]).then_inc(mix_step, 1)
                g, k, live, past = late_group(m, j, 1, steady)
                if live:
                    dve.wait_ge(rstd3_step, 2 * (g + 1))
                    if past(2):
                        dve.wait_ge(stored, 16 * (g - 1))
                    for n in range(GT):
                        ins = dve.tensor_scalar(o3[:, k, n], res3[:, k, n], mv3[:, k, n, 0:1], rstd3[:, k, n:n + 1],
                                                ALU.subtract, ALU.mult)
                    ins.then_inc(out_ready, 1)

            group_slots(dve, group_slot)


_CONSTANTS = ("rope", "eye", "before", "ones", "iota8", "base8")


def arrange(inputs):
    g = {k.split("_", 1)[1]: np.asarray(v) for k, v in inputs.items()}
    x = g["attn_x"].reshape(T, P, D)
    wup = g["attn_Wup"].reshape(LAT, H, 2, DH).transpose(0, 2, 1, 3).reshape(LAT, 2 * D)
    bup = g["attn_bup"].reshape(H, 2, DH).transpose(1, 0, 2).reshape(2 * D)

    def rows(a, n):
        return np.broadcast_to(a, (P, n))

    def chunks(a):
        return a.reshape(NC, P, -1).transpose(1, 0, 2)

    d = {
        "x": x,
        "xT": x.reshape(T, P, NC, P).transpose(0, 3, 2, 1),
        "wq": chunks(g["attn_Wq"]),
        "wdown": chunks(g["attn_Wdown"]),
        "bdown": g["attn_bdown"].reshape(LAT, 1),
        "wup": wup,
        "qk_bias": rows(np.concatenate([g["attn_bq"], bup[0:D]]), 2 * D),
        "v_bias": rows(bup[D:], D),
        "wout": chunks(g["attn_Wout"]),
        "bout": rows(g["attn_bout"], D),
        "wg": chunks(g["ffn_Wg"].T),
        "w1": g["ffn_W1"].transpose(0, 2, 1).reshape(E, NC, P, 2 * HID).transpose(0, 2, 1, 3).reshape(E, P, NC * 2 * HID),
        "b1": g["ffn_b1"].reshape(E, 2, HID // P, P).transpose(3, 0, 1, 2),
        "wo": g["ffn_Wo"].T.reshape(HID // P, P, D).transpose(1, 0, 2),
        "bo": rows(g["ffn_bo"], D),
    }
    d.update(shape_constants())
    return {k: np.ascontiguousarray(v) for k, v in d.items()}


def kernel(**inputs):
    import concourse.bacc as _bacc
    from concourse.bass_utils import run_bass_kernel_spmd as _run

    nc = _bacc.Bacc("TRN2", target_bir_lowering=False, num_devices=1)
    arrays, args = {}, {}
    for name, a in arrange(inputs).items():
        arrays[f"in_{name}_dram"] = a
        args[name] = nc.dram_tensor(f"in_{name}_dram", a.shape, mybir.dt.from_np(a.dtype), kind="ExternalInput").ap()
    out = nc.dram_tensor("out_0_dram", (N, D), F32, kind="ExternalOutput").ap()
    postln_kernel(nc, args, out)
    r = _run(nc, [arrays], core_ids=[0])
    return r.results[0]["out_0_dram"].reshape(4, 1024, D)
```

```python
from contextlib import ExitStack

import numpy as np

import concourse.bass as bass
from concourse import mybir

F32 = mybir.dt.float32
BF16 = mybir.dt.bfloat16
U32 = mybir.dt.uint32
I32 = mybir.dt.int32
ALU = mybir.AluOpType
ACT = mybir.ActivationFunctionType
AX = mybir.AxisListType

P = 128
N, D = 4096, 256
NC = D // P
H, DH = 16, 16
HG = H * H
LAT = 64
E, HID = 8, 512
TOPK = 2
T = N // P
GT = 4
NG = T // GT
U = 2 * GT
BR = 256
CAP = N + BR
NB = N * TOPK // BR + E - 1
ZROW = E * CAP
ROWS = ZROW + BR
LN_EPS, GATE_EPS = 1e-5, 1e-9
QUARTER = DH ** -0.5

DS = 7
HS = 10


def shape_constants():
    inv = (np.float32(1.0) / np.power(np.float32(10000.0), np.arange(0, DH, 2, dtype=np.float32) / np.float32(DH))).astype(np.float32)
    ang = np.arange(1024, dtype=np.float32)[:, None] * inv[None, :]
    cos, sin = np.cos(ang).astype(np.float32), np.sin(ang).astype(np.float32)
    rope = np.stack([np.concatenate([cos, cos], 1), np.concatenate([-sin, sin], 1)], 1)
    rope = rope.reshape(U, P, 2 * DH).transpose(1, 0, 2)
    return {
        "rope": np.ascontiguousarray(rope),
        "eye": np.eye(P, dtype=np.float32),
        "before": np.triu(np.ones((P, P), np.float32), 1),
        "ones": np.ones((P, P), np.float32),
        "iota8": np.ascontiguousarray(np.broadcast_to(np.arange(E, dtype=np.float32), (P, E))),
        "base8": np.ascontiguousarray(np.broadcast_to(np.arange(E, dtype=np.float32) * CAP, (P, E))),
        "iotab": np.ascontiguousarray(np.broadcast_to(np.arange(NB, dtype=np.float32), (P, NB))),
    }


def bc(ap, shape):
    return ap.broadcast_to(shape)


def postln_kernel(nc, d, out):
    with ExitStack() as ctx:
        def sb(name, shape, dt=F32):
            return ctx.enter_context(nc.sbuf_tensor(name, shape, dt))

        def psum(name, shape):
            return ctx.enter_context(nc.psum_tensor(name, shape, F32))

        def sem(name):
            return ctx.enter_context(nc.semaphore(name))

        routed_x = nc.dram_tensor("routed_x", (ROWS, D), F32, kind="Internal").ap()
        x1_dram = nc.dram_tensor("x1_dram", (T, P, D), F32, kind="Internal").ap()
        routed_y = nc.dram_tensor("routed_y", (NB * BR, D), F32, kind="Internal").ap()

        eye = sb("eye", [P, P])
        before = sb("before", [P, P])
        ones = sb("ones_sb", [P, P])
        before_b = sb("before_b", [P, P], BF16)
        ones_b = sb("ones_b", [P, P], BF16)
        iota8 = sb("iota8", [P, E])
        base8 = sb("base8", [P, E])
        rope = sb("rope", [P, U, 2 * DH])
        wq = sb("wq", [P, NC, D])
        wdown = sb("wdown", [P, NC, LAT])
        bdown = sb("bdown", [LAT, 1])
        wup = sb("wup", [LAT + 1, 2 * D])
        bq = sb("bq", [1, D])
        wout = sb("wout", [P, NC, D])
        bout = sb("bout", [P, D])
        wg = sb("wg", [P, NC, E])
        w1_hi = sb("w1_hi", [P, E, NC * 2 * HID], BF16)
        w1_lo = sb("w1_lo", [P, E, NC * 2 * HID], BF16)
        comb = sb("comb", [P, T, TOPK])
        pos_x = sb("pos_x", [P, T, TOPK])
        choice = sb("choice", [P, T, TOPK])
        pos = sb("pos", [P, T, TOPK], U32)
        shift = sb("shift", [P, T * TOPK])
        run = sb("run", [P, E])

        stage1 = ctx.enter_context(ExitStack())

        def sb1(name, shape, dt=F32):
            return stage1.enter_context(nc.sbuf_tensor(name, shape, dt))

        w1_raw = sb1("w1_raw", [P, NC * 2 * HID])
        xt = sb1("xt", [P, GT, NC, P])
        xtok = sb1("xtok", [P, GT, D])
        x1 = sb1("x1", [P, U, D])
        lat = sb1("lat", [LAT + 1, 2, P])
        qk_cos = sb1("qk_cos", [P, 2 * D])
        qk_sin = sb1("qk_sin", [P, 2 * D])
        qkr = sb1("qkr", [P, 2, 2 * D])
        v = sb1("v", [P, GT, D])
        sprod = sb1("sprod", [P, 2, DH, HG])
        smax = sb1("smax", [P, H])
        sdiff = sb1("sdiff", [P, 2, HG])
        probs = sb1("probs", [P, 2, HG])
        zsum = sb1("zsum", [P, H])
        zinv = sb1("zinv", [P, H])
        vprod = sb1("vprod", [P, HG, H])
        osum = sb1("osum", [P, D])
        onorm = sb1("onorm", [P, 2, D])
        ot = sb1("ot", [P, NC, P])
        res = sb1("res", [P, 2, D])
        stats = sb1("stats", [P, 6])
        mv = sb1("mv", [P, 2, 2])
        veps = sb1("veps", [P, 2])
        mhalf = sb1("mhalf", [P, 1])
        rstd = sb1("rstd", [P, 2])
        x1t = sb1("x1t", [P, NC, P])
        gmax = sb1("gmax", [P, GT])
        gdiff = sb1("gdiff", [P, GT, E])
        gexp = sb1("gexp", [P, GT, E])
        gz = sb1("gz", [P, GT])
        gzinv = sb1("gzinv", [P, GT])
        score = sb1("score", [P, GT, E])
        top = sb1("top", [P, GT, 8])
        topi = sb1("topi", [P, GT, 8], U32)
        topf = sb1("topf", [P, GT, TOPK])
        vsum = sb1("vsum", [P, GT])
        vinv = sb1("vinv", [P, GT])
        onehot = sb1("onehot", [P, GT, TOPK, E])
        member = sb1("member", [P, GT, E], BF16)
        pos8 = sb1("pos8", [P, GT, E])
        pos_sel = sb1("pos_sel", [P, GT, TOPK, E])
        posf = sb1("posf", [P, GT, TOPK])
        posi = sb1("posi", [P, 2, GT, TOPK], U32)

        count = sb("count", [P, E])
        count_i = sb("count_i", [P, E], I32)
        blocks_i = sb("blocks_i", [P, E], I32)
        blocks = sb("blocks", [P, E])
        blocks_to = sb("blocks_to", [P, E])
        first_row = sb("first_row", [P, E])
        expert_raw = sb("expert_raw", [P, NB])
        expert = sb("expert", [P, NB])
        row = sb("row", [P, NB])
        unused = sb("unused", [P, NB])
        row_fix = sb("row_fix", [P, NB])
        iotab = sb("iotab", [P, NB])
        tab_expert = sb("tab_expert", [P, NB], I32)
        tab_row = sb("tab_row", [P, NB], I32)
        tab_end = sb("tab_end", [P, E], I32)
        zeros = sb("zeros", [P, BR // P, D])

        CH = HID // P
        b1 = sb("b1", [P, E, 2, CH])
        wo_raw = sb("wo_raw", [P, CH, D])
        wo_hi = sb("wo_hi", [P, CH, D], BF16)
        wo_lo = sb("wo_lo", [P, CH, D], BF16)
        xrow = sb("xrow", [P, 3, BR // P, D])
        eye_b = sb("eye_b", [P, P], BF16)
        xts = sb("xts", [P, 3, 2, NC, BR], BF16)

        pick = sb("pick", [P, 2, GT, TOPK], U32)
        bo = sb("bo", [P, D])
        stats3 = sb("stats3", [P, GT, 6])
        mv3 = sb("mv3", [P, 2, GT, 2])
        veps3 = sb("veps3", [P, GT])
        mhalf3 = sb("mhalf3", [P, GT])
        eps3 = sb("eps3", [P, GT])
        rstd3 = sb("rstd3", [P, 2, GT])

        sprod_all = sprod[:].rearrange("p b d n -> p (b d n)")
        vprod_all = vprod[:].rearrange("p a g -> p (a g)")
        sig = sprod_all[:, 0:1024].rearrange("p (c n) -> p c n", c=CH)
        gated = sprod_all[:, 1024:2048].rearrange("p (c n) -> p c n", c=CH)
        g_hi = sprod_all[:, 2048:3584].bitcast(BF16).rearrange("p (b c n) -> p b c n", b=3, c=CH)
        g_lo = sprod_all[:, 3584:5120].bitcast(BF16).rearrange("p (b c n) -> p b c n", b=3, c=CH)
        yg = sprod_all[:, 4096:8192].rearrange("p (b t s n) -> p b t s n", b=2, t=GT, s=TOPK)
        yrow = sprod_all[:, 5120:6656].rearrange("p (b r n) -> p b r n", b=3, r=BR // P)
        xr = x1[:].rearrange("p (b t) n -> p b t n", b=2)
        xsplit = w1_raw[:, 0:1536].bitcast(BF16).rearrange("p (b s n) -> p b s n", b=3, s=2)
        passed = vprod_all[:, 0:NB * E].rearrange("p (b e) -> p b e", e=E)
        is_expert = vprod_all[:, 512:512 + NB * E].rearrange("p (b e) -> p b e", e=E)
        of_expert = vprod_all[:, 1024:1024 + T * TOPK * E].rearrange("p (k e) -> p k e", e=E)
        res3 = vprod_all[:, 0:2048].rearrange("p (b t n) -> p b t n", b=2, t=GT)
        o3 = vprod_all[:, 2048:4096].rearrange("p (b t n) -> p b t n", b=2, t=GT)

        ps_qk = psum("ps_qk", [P, 512])
        ps_v = psum("ps_v", [P, 512])
        ps_s = psum("ps_s", [P, 512])
        ps_t = psum("ps_t", [P, 512])
        ps_o = psum("ps_o", [P, 512])
        ps_y = psum("ps_y", [P, 512])
        ps_g = psum("ps_g", [P, 512])
        ps_r = psum("ps_r", [P, 512])
        ps_lat = ps_v[0:LAT, D:D + P]
        ps_xt = ps_o[:].bitcast(BF16)
        logits = ps_g[:, 0:GT * E].rearrange("p (t e) -> p t e", e=E)
        ps_pos = ps_r[:, 0:GT * E].rearrange("p (t e) -> p t e", e=E)
        ps_tot = ps_r[:, GT * E:(GT + 1) * E]

        w_in, wq_in, before_in = sem("w_in"), sem("wq_in"), sem("before_in")
        x_in = [sem(f"x_in{k}") for k in range(GT)]
        xt_in = [sem(f"xt_in{k}") for k in range(GT)]
        w1_in = sem("w1_in")
        lat_ready, lat_copied = sem("lat_ready"), sem("lat_copied")
        qkv_ready, qk_taken = sem("qkv_ready"), sem("qk_taken")
        rope_step = sem("rope_step")
        sprod_dve, sprod_pool = sem("sprod_dve"), sem("sprod_pool")
        scores_ready, sm_step = sem("scores_ready"), sem("sm_step")
        exp_ready = sem("exp_ready")
        vprod_dve, vprod_pool = sem("vprod_dve"), sem("vprod_pool")
        norm_step = sem("norm_step")
        ot_ready, ot_copied = sem("ot_ready"), sem("ot_copied")
        y_ready, ln_step = sem("y_ready"), sem("ln_step")
        xb_ready, rstd_ready, x1_ready = sem("xb_ready"), sem("rstd_ready"), sem("x1_ready")
        v_copied, lat_ones, count_consts, consts_in = sem("v_copied"), sem("lat_ones"), sem("count_consts"), sem("consts_in")
        x1t_ready, x1t_copied, x1_stored = sem("x1t_ready"), sem("x1t_copied"), sem("x1_stored")
        logits_ready, gexp_ready, route_step = sem("logits_ready"), sem("gexp_ready"), sem("route_step")
        count_ready = sem("count_ready")
        w1_hi_done, w1_lo_done = sem("w1_hi_done"), sem("w1_lo_done")
        const_set = sem("const_set")
        scattered, pos_kept = sem("scattered"), sem("pos_kept")
        stored = [sem(f"stored{k}") for k in range(2)]
        waits_met = sem("waits_met")
        w2_in = sem("w2_in")
        table_step, zeros_set, tails_zeroed = sem("table_step"), sem("zeros_set"), sem("tails_zeroed")
        wo_hi_done, wo_lo_done = sem("wo_hi_done"), sem("wo_lo_done")
        xrow_in = [sem(f"xrow_in{k}") for k in range(3)]
        x_hi_done, x_lo_done = sem("x_hi_done"), sem("x_lo_done")
        xrow_t, xt_copied, eye_b_set = sem("xrow_t"), sem("xt_copied"), sem("eye_b_set")
        hidden_ready, sig_ready, g_step = sem("hidden_ready"), sem("sig_ready"), sem("g_step")
        yrow_ready, yrow_copied, yrow_biased = sem("yrow_ready"), sem("yrow_copied"), sem("yrow_biased")
        yrow_out = [sem(f"yrow_out{k}") for k in range(3)]
        picked = sem("picked")
        gathered = [[sem(f"gathered{k}{n}") for n in range(GT)] for k in range(2)]
        xr_in = [[sem(f"xr_in{k}{n}") for n in range(GT)] for k in range(2)]
        mixed_first, mixed = sem("mixed_first"), sem("mixed")
        stats_ready, mv_ready = sem("stats_ready"), sem("mv_ready")
        rstd3_step, out_ready = sem("rstd3_step"), sem("out_ready")

        ROPE, SM, NORM, LN, ROUTE = 3, 2, 4, 4, 25
        WEIGHT_LOADS = 5
        CONST_LOADS = 7
        LATE_LOADS = 4
        TABLE = 24
        GATED = 3 * CH
        hidden_bank = [ps_qk, ps_v, ps_s, ps_t]

        block = ctx.enter_context(nc.Block())

        def after_waits(eng):
            eng.sem_inc(waits_met, 1)

        def slots(eng, slot):
            for j in range(U):
                slot(0, j, False)
            with eng.Fori(1, T // U) as m:
                for j in range(U):
                    slot(m, j, True)
            for j in range(U):
                slot(T // U, j, False)

        def tile_of(m, j, lag, steady):
            lag += 2
            t = m * U + (j - lag)
            return t, (j - lag) % U, steady or 0 <= t < T, (lambda k: steady or t >= k)

        def rounds(m, j, lag):
            return m * 2 + (j - lag - 2) // GT + 1

        def group_of(m, j, steady):
            q = m * 2 + (j - 11) // GT
            return q, ((j - 11) // GT) % 2, j % GT == 3 and (steady or 0 <= q < NG), (lambda k: steady or q >= k)

        def block_slots(eng, slot):
            for m in range(2):
                for j in range(3):
                    slot(m, j, False)
            with eng.Fori(2, NB // 3) as m:
                for j in range(3):
                    slot(m, j, True)
            for j in range(3):
                slot(NB // 3, j, False)

        def block_of(m, j, lag, steady):
            t = m * 3 + (j - lag)
            return t, (j - lag) % 3, steady or 0 <= t < NB, (lambda k: steady or t >= k)

        def group_slots(eng, slot):
            for m in range(2):
                for j in range(2):
                    slot(m, j, False)
            with eng.Fori(2, NG // 2) as m:
                for j in range(2):
                    slot(m, j, True)
            slot(NG // 2, 0, False)

        def late_group(m, j, lag, steady):
            g = m * 2 + (j - lag)
            return g, (j - lag) % 2, steady or 0 <= g < NG, (lambda k: steady or g >= k)

        @block.sync
        def _(sp):
            for name, buf in (("wdown", wdown), ("wup", wup), ("bdown", bdown), ("bq", bq), ("rope", rope)):
                sp.dma_start(buf[:], d[name]).then_inc(w_in, 16)
                if name == "wdown":
                    sp.dma_start(xt[:, 1], d["xT"][1]).then_inc(xt_in[1], 16)
            for t in range(2, GT):
                sp.dma_start(xt[:, t], d["xT"][t]).then_inc(xt_in[t], 16)

            def slot(m, j, steady):
                t, jt, live, past = tile_of(m, j, 0, steady)
                if live:
                    if past(GT):
                        sp.wait_ge(ln_step, LN * (t - GT) + 1)
                    sp.dma_start(xtok[:, jt % GT], d["x"][t]).then_inc(x_in[jt % GT], 16)
                t, jt, live, past = tile_of(m, j, -2, steady)
                if live and past(GT):
                    sp.wait_ge(qkv_ready, t - GT + 1)
                    sp.dma_start(xt[:, jt % GT], d["xT"][t]).then_inc(xt_in[jt % GT], 16)
                t, jt, live, past = tile_of(m, j, 4, steady)
                if live:
                    sp.wait_ge(x1_ready, t + 1)
                    sp.dma_start(x1_dram[t], x1[:, jt]).then_inc(x1_stored, 16)
                    sp.wait_ge(x1_stored, 16 * (t + 1))
                    after_waits(sp)
                if j % GT == 0 and (steady or m * 2 + j // GT < NG):
                    g = m * 2 + j // GT
                    if steady or g > 0:
                        sp.wait_ge(w1_hi_done, g)
                        sp.wait_ge(w1_lo_done, g)
                    sp.dma_start(w1_raw[:], d["w1"][g]).then_inc(w1_in, 16)

            sp.dma_start(b1[:], d["b1"]).then_inc(w2_in, 16)
            sp.dma_start(wo_raw[:], d["wo"]).then_inc(w2_in, 16)
            sp.dma_start(bo[:], d["bo"]).then_inc(w2_in, 16)
            sp.dma_start(iotab[:], d["iotab"]).then_inc(w2_in, 16)
            slots(sp, slot)
            sp.wait_ge(zeros_set, 1)
            sp.dma_start(routed_x[ZROW:ZROW + BR].rearrange("(r p) d -> p r d", p=P), zeros[:]).then_inc(tails_zeroed, 16)
            sp.wait_ge(scattered, 16 + 16 * T * TOPK)
            sp.wait_ge(table_step, 1)
            for e in range(E):
                end = sp.value_load(tab_end[0:1, e:e + 1], min_val=e * CAP, max_val=e * CAP + N)
                sp.dma_start(routed_x[bass.ds(end, BR)].rearrange("(r p) d -> p r d", p=P),
                             zeros[:]).then_inc(tails_zeroed, 16)
            sp.wait_ge(tails_zeroed, 16 * (E + 1))
            sp.wait_ge(table_step, TABLE)

            def block_slot(m, j, steady):
                b, jb, live, past = block_of(m, j, 0, steady)
                if live:
                    if past(3):
                        sp.wait_ge(x_lo_done, b - 2)
                    src = sp.value_load(tab_row[0:1, bass.ds(b, 1)], min_val=0, max_val=ROWS - BR)
                    sp.dma_start(xrow[:, jb], routed_x[bass.ds(src, BR)].rearrange("(r p) d -> p r d", p=P)
                                 ).then_inc(xrow_in[jb], 16)
                b, jb, live, past = block_of(m, j, 3, steady)
                if live:
                    sp.wait_ge(yrow_biased, b + 1)
                    sp.dma_start(routed_y.rearrange("(b r p) d -> b p r d", p=P, r=BR // P)[b], yrow[:, jb]
                                 ).then_inc(yrow_out[jb], 16)

            block_slots(sp, block_slot)

            def group_slot(m, j, steady):
                g, k, live, past = late_group(m, j, 0, steady)
                if live:
                    for n in range(GT):
                        if past(2):
                            sp.wait_ge(mixed_first, GT * (g - 2) + n + 1)
                        sp.dma_start(xr[:, k, n], x1_dram[g * GT + n]).then_inc(xr_in[k][n], 16)

            group_slots(sp, group_slot)
            for k in range(2):
                sp.wait_ge(stored[k], 16 * NG // 2)

        @block.tensor
        def _(pe):
            def latent(m, j, t, jt, past):
                pe.wait_ge(xt_in[jt % GT], 16 * rounds(m, j, -2))
                if past(1):
                    pe.wait_ge(lat_copied, t)
                if past(2):
                    pe.wait_ge(v_copied, t - 1)
                for c in range(NC):
                    mm = pe.matmul(ps_lat, wdown[:, c], xt[:, jt % GT, c], start=(c == 0), stop=(c == NC - 1))
                mm.then_inc(lat_ready, 1)

            def qkv(t, jt, past):
                pe.wait_ge(lat_copied, t + 1)
                if past(1):
                    pe.wait_ge(qk_taken, t)
                for c in range(NC):
                    pe.matmul(ps_qk[:, 0:D], xt[:, jt % GT, c], wq[:, c], start=(c == 0), stop=False)
                pe.matmul(ps_qk[:, 0:D], ones[0:1, :], bq[:], start=False, stop=True)
                pe.matmul(ps_qk[:, D:2 * D], lat[:, jt % 2], wup[:, 0:D], start=True, stop=True)
                pe.matmul(ps_v[:, 0:D], lat[:, jt % 2], wup[:, D:2 * D], start=True, stop=True).then_inc(qkv_ready, 1)

            pe.wait_ge(w_in, 16 * WEIGHT_LOADS)
            pe.wait_ge(wq_in, 16)
            pe.wait_ge(consts_in, 16 * CONST_LOADS)
            pe.wait_ge(lat_ones, 1)
            pe.wait_ge(count_consts, 2)

            def slot(m, j, steady):
                t, jt, live, past = tile_of(m, j, 3, steady)
                if live:
                    pe.wait_ge(norm_step, NORM * (t + 1))
                    if past(1):
                        pe.wait_ge(ot_copied, t)
                    if past(3):
                        pe.wait_ge(x1t_copied, t - 2)
                    for c in range(NC):
                        tr = pe.transpose(ps_t[:, c * P:(c + 1) * P], onorm[:, jt % 2, c * P:(c + 1) * P], eye[:])
                    tr.then_inc(ot_ready, 1)
                t, jt, live, past = tile_of(m, j, 5, steady)
                if live:
                    pe.wait_ge(x1_ready, t + 1)
                    if past(1):
                        pe.wait_ge(x1t_copied, t)
                    if not steady:
                        pe.wait_ge(ot_copied, min(t + 2, T))
                    for c in range(NC):
                        tr = pe.transpose(ps_t[:, D + c * P:D + (c + 1) * P], x1[:, jt, c * P:(c + 1) * P], eye[:])
                    tr.then_inc(x1t_ready, 1)
                t, jt, live, past = tile_of(m, j, 3, steady)
                if live:
                    pe.wait_ge(ot_copied, t + 1)
                    if past(1):
                        pe.wait_ge(ln_step, LN * (t - 1) + 1)
                    for c in range(NC):
                        mm = pe.matmul(ps_y[:, 0:D], ot[:, c], wout[:, c], start=(c == 0), stop=(c == NC - 1))
                    mm.then_inc(y_ready, 1)
                q, k, live, past = group_of(m, j, steady)
                if live:
                    pe.wait_ge(route_step, ROUTE * q + 19)
                    for k in range(GT):
                        for kk in range(k):
                            pe.matmul(ps_pos[:, k], ones_b[:], member[:, kk], start=(kk == 0), stop=False)
                        pe.matmul(ps_pos[:, k], before_b[:], member[:, k], start=(k == 0), stop=True)
                    for k in range(GT):
                        mm = pe.matmul(ps_tot, ones_b[:], member[:, k], start=(k == 0), stop=(k == GT - 1))
                    mm.then_inc(count_ready, 1)
                t, jt, live, past = tile_of(m, j, 1, steady)
                if live:
                    b = jt % 2
                    pe.wait_ge(sprod_dve, t + 1)
                    pe.wait_ge(sprod_pool, t + 1)
                    if past(1):
                        pe.wait_ge(sm_step, SM * t)
                    for k in range(DH):
                        mm = pe.matmul(ps_s[:, 0:HG], eye[:], sprod[:, b, k], start=(k == 0), stop=(k == DH - 1))
                    mm.then_inc(scores_ready, 1)
                t, jt, live, past = tile_of(m, j, -2, steady)
                if live:
                    latent(m, j, t, jt, past)
                t, jt, live, past = tile_of(m, j, -1, steady)
                if live:
                    qkv(t, jt, past)
                t, jt, live, past = tile_of(m, j, 5, steady)
                if live:
                    pe.wait_ge(x1t_copied, t + 1)
                    if jt % GT == 0 and past(GT):
                        pe.wait_ge(route_step, ROUTE * (rounds(m, j, 5) - 2) + 2)
                    for c in range(NC):
                        mm = pe.matmul(logits[:, jt % GT], x1t[:, c], wg[:, c], start=(c == 0), stop=(c == NC - 1))
                    mm.then_inc(logits_ready, 1)

            slots(pe, slot)
            pe.wait_ge(w1_hi_done, E)
            pe.wait_ge(w1_lo_done, E)
            pe.wait_ge(wo_hi_done, 1)
            pe.wait_ge(wo_lo_done, 1)
            pe.wait_ge(eye_b_set, 1)
            pe.wait_ge(table_step, TABLE)
            pe.wait_ge(gexp_ready, NG)

            def block_slot(m, j, steady):
                b, jb, live, past = block_of(m, j, 2, steady)
                if live:
                    e = pe.value_load(tab_expert[0:1, bass.ds(b, 1)], min_val=0, max_val=E - 1)
                    pe.wait_ge(xt_copied, b + 1)
                    for c in range(CH):
                        if past(1):
                            pe.wait_ge(g_step, GATED * (b - 1) + 3 * c + 1)
                        for half in range(2):
                            n = 0
                            for w, x in ((w1_hi, 0), (w1_hi, 1), (w1_lo, 0)):
                                for kc in range(NC):
                                    at = kc * 2 * HID + half * HID + c * P
                                    mm = pe.matmul(hidden_bank[c][:, half * BR:(half + 1) * BR],
                                                   w[:, bass.ds(e, 1), at:at + P].rearrange("p o n -> p (o n)"), xts[:, jb, x, kc],
                                                   start=(n == 0), stop=(n == 5))
                                    n += 1
                        mm.then_inc(hidden_ready, 1)
                b, jb, live, past = block_of(m, j, 1, steady)
                if live:
                    pe.wait_ge(x_hi_done, b + 1)
                    pe.wait_ge(x_lo_done, b + 1)
                    if past(1):
                        pe.wait_ge(xt_copied, b)
                    for s in range(2):
                        for r in range(BR // P):
                            for c in range(NC):
                                at = (s * NC + c) * BR + r * P
                                tr = pe.transpose(ps_xt[:, at:at + P], xsplit[:, jb, s, r * D + c * P:r * D + (c + 1) * P],
                                                  eye_b[:])
                    tr.then_inc(xrow_t, 1)
                b, jb, live, past = block_of(m, j, 3, steady)
                if live:
                    if past(1):
                        pe.wait_ge(yrow_copied, b)
                    pe.wait_ge(g_step, GATED * (b + 1))
                    for r in range(BR // P):
                        n = 0
                        for c in range(CH):
                            for gg, w in ((g_hi, wo_hi), (g_lo, wo_hi), (g_hi, wo_lo)):
                                mm = pe.matmul(ps_y[:, r * D:(r + 1) * D], gg[:, jb, c, r * P:(r + 1) * P], w[:, c],
                                               start=(n == 0), stop=(n == 3 * CH - 1))
                                n += 1
                    mm.then_inc(yrow_ready, 1)

            block_slots(pe, block_slot)

        @block.scalar
        def _(act):
            act.dma_start(xt[:, 0], d["xT"][0]).then_inc(xt_in[0], 16)
            act.dma_start(wq[:], d["wq"]).then_inc(wq_in, 16)
            for name, buf in (("eye", eye), ("wout", wout), ("bout", bout), ("wg", wg), ("iota8", iota8),
                              ("base8", base8), ("base8", run)):
                act.dma_start(buf[:], d[name]).then_inc(consts_in, 16)
            act.wait_ge(w_in, 16 * WEIGHT_LOADS)

            def copy_latent(t, jt, past):
                act.wait_ge(lat_ready, t + 1)
                if past(2):
                    act.wait_ge(qkv_ready, t - 1)
                act.activation(lat[0:LAT, jt % 2], ps_lat, ACT.Identity, bias=bdown[:]).then_inc(lat_copied, 1)


            def slot(m, j, steady):
                q, k, live, past = group_of(m, j, steady)
                if live:
                    act.wait_ge(route_step, ROUTE * q + 2)
                    act.activation(gexp[:], gdiff[:], ACT.Exp).then_inc(gexp_ready, 1)
                t, jt, live, past = tile_of(m, j, 3, steady)
                if live:
                    act.wait_ge(ot_ready, t + 1)
                    if past(2):
                        act.wait_ge(x1t_ready, t - 1)
                    if past(1):
                        act.wait_ge(y_ready, t)
                    act.copy(ot[:].rearrange("p c k -> p (c k)"), ps_t[:, 0:D]).then_inc(ot_copied, 1)
                t, jt, live, past = tile_of(m, j, 5, steady)
                if live:
                    act.wait_ge(x1t_ready, t + 1)
                    if past(1):
                        act.wait_ge(logits_ready, t)
                    act.copy(x1t[:].rearrange("p c k -> p (c k)"), ps_t[:, D:2 * D]).then_inc(x1t_copied, 1)
                if j % GT == 2 and (steady or m * 2 + j // GT < NG):
                    g = m * 2 + j // GT
                    act.wait_ge(w1_in, 16 * (g + 1))
                    act.copy(w1_hi[:, g], w1_raw[:]).then_inc(w1_hi_done, 1)
                t, jt, live, past = tile_of(m, j, -2, steady)
                if live:
                    if past(1):
                        act.wait_ge(qkv_ready, t)
                    copy_latent(t, jt, past)
                t, jt, live, past = tile_of(m, j, -1, steady)
                if live:
                    act.wait_ge(qkv_ready, t + 1)
                    if past(GT):
                        act.wait_ge(vprod_dve, t - GT + 1)
                        act.wait_ge(vprod_pool, t - GT + 1)
                    act.copy(v[:, jt % GT], ps_v[:, 0:D]).then_inc(v_copied, 1)
                t, jt, live, past = tile_of(m, j, 1, steady)
                if live:
                    act.wait_ge(sm_step, SM * (t + 1))
                    if past(2):
                        act.wait_ge(norm_step, NORM * (t - 1))
                        act.wait_ge(vprod_pool, t - 1)
                    act.activation(probs[:, jt % 2], sdiff[:, jt % 2], ACT.Exp, scale=QUARTER).then_inc(exp_ready, 1)

            slots(act, slot)
            act.wait_ge(w2_in, 16 * LATE_LOADS)
            act.copy(wo_hi[:], wo_raw[:]).then_inc(wo_hi_done, 1)
            act.copy(eye_b[:], eye[:]).then_inc(eye_b_set, 1)
            act.wait_ge(table_step, TABLE)

            def block_slot(m, j, steady):
                b, jb, live, past = block_of(m, j, 1, steady)
                if live:
                    act.wait_ge(xrow_in[jb], 16 * (m + (j - 1) // 3 + 1))
                    if past(3):
                        act.wait_ge(xrow_t, b - 2)
                    act.copy(xsplit[:, jb, 0], xrow[:, jb].rearrange("p r n -> p (r n)")).then_inc(x_hi_done, 1)
                b, jb, live, past = block_of(m, j, 2, steady)
                if live:
                    e = act.value_load(tab_expert[0:1, bass.ds(b, 1)], min_val=0, max_val=E - 1)
                    for c in range(CH):
                        act.wait_ge(hidden_ready, CH * b + c + 1)
                        if past(1):
                            act.wait_ge(g_step, GATED * (b - 1) + 3 * c + 1)
                        act.activation(sig[:, c], hidden_bank[c][:, BR:2 * BR], ACT.Sigmoid,
                                       bias=b1[:, bass.ds(e, 1), 1, c:c + 1].rearrange("p o n -> p (o n)")).then_inc(sig_ready, 1)
                b, jb, live, past = block_of(m, j, 1, steady)
                if live:
                    act.wait_ge(xrow_t, b + 1)
                    if past(3):
                        act.wait_ge(hidden_ready, CH * (b - 2))
                    act.copy(xts[:, jb].rearrange("p s c n -> p (s c n)"), ps_xt).then_inc(xt_copied, 1)
                b, jb, live, past = block_of(m, j, 3, steady)
                if live:
                    act.wait_ge(yrow_ready, b + 1)
                    if past(3):
                        act.wait_ge(yrow_out[jb], 16 * (m + (j - 3) // 3))
                    act.copy(yrow[:, jb].rearrange("p r n -> p (r n)"), ps_y[:]).then_inc(yrow_copied, 1)

            block_slots(act, block_slot)

            def group_slot(m, j, steady):
                g, k, live, past = late_group(m, j, 1, steady)
                if live:
                    act.wait_ge(out_ready, g + 1)
                    act.dma_start(out.rearrange("(g n p) d -> g p n d", p=P, n=GT)[g], o3[:, k]).then_inc(stored[k], 16)

            act.wait_ge(table_step, TABLE)
            group_slots(act, group_slot)

        @block.gpsimd
        def _(pool):
            pool.dma_start(before[:], d["before"]).then_inc(before_in, 16)
            pool.dma_start(ones[:], d["ones"]).then_inc(scattered, 16)
            pool.memset(mhalf[:], -0.5).then_inc(const_set, 1)
            pool.wait_ge(const_set, 1)
            pool.memset(lat[LAT:LAT + 1], 1.0).then_inc(lat_ones, 1)
            pool.wait_ge(lat_ones, 1)
            pool.wait_ge(before_in, 16)
            pool.wait_ge(scattered, 16)
            pool.tensor_copy(before_b[:], before[:]).then_inc(count_consts, 1)
            pool.tensor_copy(ones_b[:], ones[:]).then_inc(count_consts, 1)

            def slot(m, j, steady):
                if j % GT == 1 and (steady or 0 <= m * 2 + (j - 13) // GT < NG):
                    pool.wait_ge(scattered, 16 + 16 * GT * TOPK * (m * 2 + (j - 13) // GT + 1))
                t, jt, live, past = tile_of(m, j, 2, steady)
                if live:
                    b = jt % 2
                    pool.wait_ge(exp_ready, t + 1)
                    pool.wait_ge(v_copied, t + 1)
                    if past(1):
                        pool.wait_ge(norm_step, NORM * (t - 1) + 3)
                    n = H - HS
                    pool.tensor_tensor(
                        vprod[:, HS * DH:].rearrange("p (h d) g -> p h d g", h=n),
                        probs[:, b, HS * H:].rearrange("p (h o g) -> p h o g", h=n, o=1).broadcast_to([P, n, DH, H]),
                        v[:, jt % GT].rearrange("p (o g d) -> p o d g", o=1, g=H).broadcast_to([P, n, DH, H]),
                        ALU.mult).then_inc(vprod_pool, 1)
                t, jt, live, past = tile_of(m, j, 0, steady)
                if live:
                    b = jt % 2
                    pool.wait_ge(rope_step, ROPE * (t + 1))
                    if past(2):
                        pool.wait_ge(scores_ready, t - 1)
                    n = DH - DS
                    qr = qkr[:, b, 0:D].rearrange("p (h o d) -> p d h o", h=H, o=1)[:, DS:].broadcast_to([P, n, H, H])
                    kr = qkr[:, b, D:2 * D].rearrange("p (o g d) -> p d o g", o=1, g=H)[:, DS:].broadcast_to([P, n, H, H])
                    pool.tensor_tensor(sprod[:, b, DS:].rearrange("p d (h g) -> p d h g", h=H), qr, kr,
                                       ALU.mult).then_inc(sprod_pool, 1)
                t, jt, live, past = tile_of(m, j, 1, steady)
                if live:
                    pool.wait_ge(x_in[jt % GT], 16 * rounds(m, j, 1))
                    pool.tensor_tensor(xtok[:, jt % GT], xtok[:, jt % GT], bout[:], ALU.add).then_inc(xb_ready, 1)
                q, k, routed, past = group_of(m, j, steady)
                if routed:
                    pool.wait_ge(route_step, ROUTE * (q + 1))
                    after_waits(pool)
                    for n in range(GT):
                        for s in range(TOPK):
                            pool.indirect_dma_start(
                                routed_x, bass.IndirectOffsetOnAxis(ap=posi[:, k, n, s:s + 1], axis=0),
                                x1[:, k * GT + n], None).then_inc(scattered, 16)
                t, jt, live, past = tile_of(m, j, 3, steady)
                if live:
                    b = jt % 2
                    pool.wait_ge(ln_step, LN * (t + 1))
                    if past(2):
                        pool.wait_ge(x1_ready, t - 1)
                    pool.tensor_tensor(rstd[:, b:b + 1], veps[:, b:b + 1], mhalf[:], ALU.pow).then_inc(rstd_ready, 1)
            slots(pool, slot)
            pool.memset(mhalf3[:], -0.5).then_inc(const_set, 1)
            pool.memset(eps3[:], LN_EPS).then_inc(const_set, 1)
            pool.wait_ge(const_set, 3)
            pool.wait_ge(w2_in, 16 * LATE_LOADS)
            pool.wait_ge(table_step, TABLE)

            def block_slot(m, j, steady):
                b, jb, live, past = block_of(m, j, 1, steady)
                if live:
                    pool.wait_ge(x_hi_done, b + 1)
                    if past(3):
                        pool.wait_ge(xrow_t, b - 2)
                    pool.tensor_tensor(xsplit[:, jb, 1], xrow[:, jb].rearrange("p r n -> p (r n)"),
                                       xsplit[:, jb, 0], ALU.subtract).then_inc(x_lo_done, 1)
                b, jb, live, past = block_of(m, j, 3, steady)
                if live:
                    pool.wait_ge(yrow_copied, b + 1)
                    pool.tensor_tensor(yrow[:, jb], yrow[:, jb],
                                       bo[:].rearrange("p (o n) -> p o n", o=1).broadcast_to([P, BR // P, D]),
                                       ALU.add).then_inc(yrow_biased, 1)

            block_slots(pool, block_slot)
            for k in range(3):
                pool.wait_ge(yrow_out[k], 16 * (NB // 3))

            def group_slot(m, j, steady):
                g, k, live, past = late_group(m, j, 0, steady)
                if live:
                    if past(2):
                        for n in range(GT):
                            pool.wait_ge(gathered[k][n], 32 * m)
                    pool.tensor_copy(pick[:, k], pos[:, bass.ds(g * GT, GT)]).then_inc(picked, 1)
                    pool.wait_ge(picked, g + 1)
                    for n in range(GT):
                        if past(2):
                            pool.wait_ge(mixed, GT * (g - 2) + n + 1)
                        after_waits(pool)
                        for s in range(TOPK):
                            pool.indirect_dma_start(
                                yg[:, k, n, s], None, routed_y,
                                bass.IndirectOffsetOnAxis(ap=pick[:, k, n, s:s + 1], axis=0)).then_inc(gathered[k][n], 16)
                g, k, live, past = late_group(m, j, 1, steady)
                if live:
                    pool.wait_ge(mv_ready, GT * (g + 1))
                    if past(1):
                        pool.wait_ge(rstd3_step, 2 * g)
                    pool.tensor_tensor(veps3[:], mv3[:, k, :, 1], eps3[:], ALU.add).then_inc(rstd3_step, 1)
                    pool.wait_ge(rstd3_step, 2 * g + 1)
                    if past(2):
                        pool.wait_ge(out_ready, g - 1)
                    pool.tensor_tensor(rstd3[:, k], veps3[:], mhalf3[:], ALU.pow).then_inc(rstd3_step, 1)

            group_slots(pool, group_slot)

        @block.vector
        def _(dve):
            dve.memset(zeros[:], 0.0).then_inc(zeros_set, 1)
            dve.wait_ge(w_in, 16 * WEIGHT_LOADS)
            dve.wait_ge(consts_in, 16 * CONST_LOADS)

            def slot(m, j, steady):
                def normalise():
                    t, jt, live, past = tile_of(m, j, 4, steady)
                    if not live:
                        return
                    b = jt % 2
                    dve.wait_ge(rstd_ready, t + 1)
                    dve.tensor_scalar(x1[:, jt], res[:, b], mv[:, b, 0:1], rstd[:, b:b + 1], ALU.subtract,
                                      ALU.mult).then_inc(x1_ready, 1)

                q, k, routed, _ = group_of(m, j, steady)
                if routed:
                    gate_scores(q)
                t, jt, live, past = tile_of(m, j, 0, steady)
                if live:
                    b = jt % 2
                    dve.wait_ge(qkv_ready, t + 1)
                    if past(1):
                        dve.wait_ge(rope_step, ROPE * t)
                    heads = 2 * H
                    qk = ps_qk[:].rearrange("p (h d) -> p h d", h=heads)
                    dve.tensor_tensor(
                        qk_cos[:].rearrange("p (h d) -> p h d", h=heads), qk,
                        rope[:, jt, 0:DH].rearrange("p (o d) -> p o d", o=1).broadcast_to([P, heads, DH]),
                        ALU.mult).then_inc(rope_step, 1)
                    for half in range(2):
                        a, z = half * DH // 2, (1 - half) * DH // 2
                        ins = dve.tensor_tensor(
                            qk_sin[:].rearrange("p (h d) -> p h d", h=heads)[:, :, a:a + DH // 2],
                            qk[:, :, z:z + DH // 2],
                            rope[:, jt, DH + a:DH + a + DH // 2].rearrange("p (o d) -> p o d", o=1)
                            .broadcast_to([P, heads, DH // 2]), ALU.mult)
                        ins.then_inc(rope_step, 1) if half == 0 else ins.then_inc(qk_taken, 1)
                normalise()
                if live:
                    dve.wait_ge(qk_taken, t + 1)
                    if past(2):
                        dve.wait_ge(sprod_pool, t - 1)
                        dve.wait_ge(sprod_dve, t - 1)
                    dve.tensor_tensor(qkr[:, b], qk_cos[:], qk_sin[:], ALU.add).then_inc(rope_step, 1)

                t2, jt2, live2, past2 = tile_of(m, j, 2, steady)
                b2 = jt2 % 2
                if live2:
                    dve.wait_ge(exp_ready, t2 + 1)
                    if past2(1):
                        dve.wait_ge(norm_step, NORM * t2)
                    dve.tensor_reduce(zsum[:], probs[:, b2].rearrange("p (h g) -> p h g", h=H), AX.X,
                                      ALU.add).then_inc(norm_step, 1)
                if routed:
                    choose(q)
                if live:
                    dve.wait_ge(rope_step, ROPE * (t + 1))
                    if past(2):
                        dve.wait_ge(scores_ready, t - 1)
                    qr = qkr[:, b, 0:D].rearrange("p (h o d) -> p d h o", h=H, o=1)[:, 0:DS].broadcast_to([P, DS, H, H])
                    kr = qkr[:, b, D:2 * D].rearrange("p (o g d) -> p d o g", o=1, g=H)[:, 0:DS].broadcast_to([P, DS, H, H])
                    dve.tensor_tensor(sprod[:, b, 0:DS].rearrange("p d (h g) -> p d h g", h=H), qr, kr,
                                      ALU.mult).then_inc(sprod_dve, 1)
                if routed:
                    take_rows(q, k)
                if live2:
                    dve.wait_ge(norm_step, NORM * t2 + 1)
                    dve.reciprocal(zinv[:], zsum[:]).then_inc(norm_step, 1)
                    dve.wait_ge(v_copied, t2 + 1)
                    dve.tensor_tensor(
                        vprod[:, 0:HS * DH].rearrange("p (h d) g -> p h d g", h=HS),
                        probs[:, b2, 0:HS * H].rearrange("p (h o g) -> p h o g", h=HS, o=1).broadcast_to([P, HS, DH, H]),
                        v[:, jt2 % GT].rearrange("p (o g d) -> p o d g", o=1, g=H).broadcast_to([P, HS, DH, H]),
                        ALU.mult).then_inc(vprod_dve, 1)

                t3, jt3, live3, past3 = tile_of(m, j, 3, steady)
                b3 = jt3 % 2
                if live3:
                    dve.wait_ge(y_ready, t3 + 1)
                    dve.wait_ge(xb_ready, t3 + 1)
                    if past3(2):
                        dve.wait_ge(x1_ready, t3 - 1)
                    if past3(1):
                        dve.wait_ge(ln_step, LN * t3)
                    dve.tensor_tensor(res[:, b3], ps_y[:, 0:D], xtok[:, jt3 % GT], ALU.add).then_inc(ln_step, 1)

                if live2:
                    dve.wait_ge(vprod_pool, t2 + 1)
                    dve.wait_ge(vprod_dve, t2 + 1)
                    dve.tensor_reduce(osum[:], vprod[:], AX.X, ALU.add).then_inc(norm_step, 1)
                if live3:
                    dve.wait_ge(ln_step, LN * t3 + 1)
                    dve.bn_stats(stats[:], res[:, b3]).then_inc(ln_step, 1)
                if live2:
                    dve.wait_ge(norm_step, NORM * t2 + 3)
                    if past2(2):
                        dve.wait_ge(ot_ready, t2 - 1)
                    dve.tensor_tensor(
                        onorm[:, b2].rearrange("p (h d) -> p h d", h=H), osum[:].rearrange("p (h d) -> p h d", h=H),
                        zinv[:].rearrange("p (h o) -> p h o", o=1).broadcast_to([P, H, DH]), ALU.mult).then_inc(norm_step, 1)
                if live3:
                    dve.wait_ge(ln_step, LN * t3 + 2)
                    if past3(2):
                        dve.wait_ge(rstd_ready, t3 - 1)
                    after_waits(dve)
                    dve.bn_aggr(mv[:, b3], stats[:]).then_inc(ln_step, 1)

                if live3:
                    dve.wait_ge(ln_step, LN * t3 + 3)
                    dve.tensor_scalar(veps[:, b3:b3 + 1], mv[:, b3, 1:2], LN_EPS, None, ALU.add).then_inc(ln_step, 1)

                t1, jt1, live1, past1 = tile_of(m, j, 1, steady)
                if live1:
                    b1 = jt1 % 2
                    dve.wait_ge(scores_ready, t1 + 1)
                    if past1(1):
                        dve.wait_ge(sm_step, SM * t1)
                    sc = ps_s[:, 0:HG].rearrange("p (h g) -> p h g", h=H)
                    dve.tensor_reduce(smax[:], sc, AX.X, ALU.max).then_inc(sm_step, 1)
                    dve.wait_ge(sm_step, SM * t1 + 1)
                    if past1(2):
                        dve.wait_ge(exp_ready, t1 - 1)
                    dve.tensor_tensor(sdiff[:, b1].rearrange("p (h g) -> p h g", h=H), sc,
                                      smax[:].rearrange("p (h o) -> p h o", o=1).broadcast_to([P, H, H]),
                                      ALU.subtract).then_inc(sm_step, 1)

                if j % GT == 2 and (steady or m * 2 + j // GT < NG):
                    g = m * 2 + j // GT
                    dve.wait_ge(w1_hi_done, g + 1)
                    dve.tensor_tensor(w1_lo[:, g], w1_raw[:], w1_hi[:, g], ALU.subtract).then_inc(w1_lo_done, 1)

            def gate_scores(q):
                at = ROUTE * q
                dve.wait_ge(logits_ready, GT * (q + 1))
                dve.tensor_reduce(gmax[:], logits[:], AX.X, ALU.max).then_inc(route_step, 1)
                dve.wait_ge(route_step, at + 1)
                dve.tensor_tensor(gdiff[:], logits[:], gmax[:].rearrange("p (t o) -> p t o", o=1).broadcast_to([P, GT, E]),
                                  ALU.subtract).then_inc(route_step, 1)

            def choose(q):
                at = ROUTE * q
                dve.wait_ge(gexp_ready, q + 1)
                dve.tensor_reduce(gz[:], gexp[:], AX.X, ALU.add).then_inc(route_step, 1)
                dve.wait_ge(route_step, at + 3)
                dve.reciprocal(gzinv[:], gz[:]).then_inc(route_step, 1)
                dve.wait_ge(route_step, at + 4)
                dve.tensor_tensor(score[:], gexp[:], gzinv[:].rearrange("p (t o) -> p t o", o=1).broadcast_to([P, GT, E]),
                                  ALU.mult).then_inc(route_step, 1)
                dve.wait_ge(route_step, at + 5)
                after_waits(dve)
                for n in range(GT):
                    dve.max(top[:, n], score[:, n]).then_inc(route_step, 1)
                dve.wait_ge(route_step, at + 9)
                after_waits(dve)
                for n in range(GT):
                    dve.max_index(topi[:, n], top[:, n], score[:, n]).then_inc(route_step, 1)
                dve.wait_ge(route_step, at + 13)
                dve.tensor_copy(topf[:], topi[:, :, 0:TOPK]).then_inc(route_step, 1)
                dve.scalar_tensor_tensor(out=vsum[:], in0=top[:, :, 0], scalar=GATE_EPS, in1=top[:, :, 1],
                                         op0=ALU.add, op1=ALU.add).then_inc(route_step, 1)
                dve.wait_ge(route_step, at + 14)
                for s in range(TOPK):
                    dve.tensor_tensor(onehot[:, :, s], iota8[:].rearrange("p (o e) -> p o e", o=1).broadcast_to([P, GT, E]),
                                      topf[:, :, s:s + 1].broadcast_to([P, GT, E]), ALU.is_equal).then_inc(route_step, 1)
                dve.wait_ge(route_step, at + 15)
                dve.reciprocal(vinv[:], vsum[:]).then_inc(route_step, 1)
                dve.wait_ge(route_step, at + 17)
                dve.tensor_tensor(member[:], onehot[:, :, 0], onehot[:, :, 1], ALU.add).then_inc(route_step, 1)
                dve.wait_ge(route_step, at + 18)
                dve.tensor_tensor(comb[:, bass.ds(q * GT, GT)], top[:, :, 0:TOPK],
                                  vinv[:].rearrange("p (t o) -> p t o", o=1).broadcast_to([P, GT, TOPK]),
                                  ALU.mult).then_inc(route_step, 1)

            def take_rows(q, k):
                at = ROUTE * q
                dve.wait_ge(count_ready, q + 1)
                run_b = run[:].rearrange("p (o e) -> p o e", o=1).broadcast_to([P, GT, E])
                dve.tensor_tensor(pos8[:], ps_pos, run_b, ALU.add).then_inc(route_step, 1)
                dve.wait_ge(route_step, at + 21)
                for s in range(TOPK):
                    ins = dve.tensor_tensor(pos_sel[:, :, s], onehot[:, :, s], pos8[:], ALU.mult)
                ins.then_inc(route_step, 1)
                dve.tensor_tensor(run[:], run[:], ps_tot, ALU.add).then_inc(route_step, 1)
                dve.wait_ge(route_step, at + 22)
                dve.tensor_reduce(posf[:], pos_sel[:], AX.X, ALU.add).then_inc(route_step, 1)
                dve.wait_ge(route_step, at + 24)
                dve.tensor_copy(posi[:, k], posf[:]).then_inc(route_step, 1)
                dve.tensor_copy(pos_x[:, bass.ds(q * GT, GT)], posf[:])
                dve.tensor_copy(choice[:, bass.ds(q * GT, GT)], topf[:]).then_inc(pos_kept, 1)

            slots(dve, slot)
            dve.wait_ge(w2_in, 16 * LATE_LOADS)
            dve.wait_ge(pos_kept, NG)
            step = 0

            def table(ins, then=True):
                nonlocal step
                step += 1
                ins.then_inc(table_step, 1)
                if then:
                    dve.wait_ge(table_step, step)

            def over_blocks(a):
                return a.rearrange("p (o e) -> p o e", o=1).broadcast_to([P, NB, E])

            def over_experts(a):
                return a.rearrange("p (b o) -> p b o", o=1).broadcast_to([P, NB, E])

            table(dve.tensor_copy(tab_end[:], run[:]), then=False)
            table(dve.tensor_tensor(count[:], run[:], base8[:], ALU.subtract))
            table(dve.tensor_scalar(count_i[:], count[:], float(BR - 1), None, ALU.add))
            table(dve.tensor_scalar(blocks_i[:], count_i[:], BR.bit_length() - 1, None, ALU.logical_shift_right))
            table(dve.tensor_copy(blocks[:], blocks_i[:]))
            table(dve.tensor_tensor_scan(blocks_to[:], ones[:, 0:E], blocks[:], 0.0, ALU.mult, ALU.add))
            table(dve.tensor_tensor(passed, over_experts(iotab[:]), over_blocks(blocks_to[:]), ALU.is_ge))
            table(dve.tensor_reduce(expert_raw[:], passed, AX.X, ALU.add))
            table(dve.tensor_scalar(expert[:], expert_raw[:], float(E - 1), None, ALU.min))
            table(dve.tensor_tensor(is_expert, over_blocks(iota8[:]), over_experts(expert[:]), ALU.is_equal))
            table(dve.tensor_tensor(first_row[:], blocks_to[:], blocks[:], ALU.subtract))
            table(dve.scalar_tensor_tensor(out=first_row[:], in0=first_row[:], scalar=-float(BR), in1=base8[:],
                                           op0=ALU.mult, op1=ALU.add))
            table(dve.tensor_tensor(passed, is_expert, over_blocks(first_row[:]), ALU.mult))
            table(dve.tensor_reduce(row[:], passed, AX.X, ALU.add))
            table(dve.scalar_tensor_tensor(out=row[:], in0=iotab[:], scalar=float(BR), in1=row[:], op0=ALU.mult, op1=ALU.add))
            table(dve.tensor_scalar(unused[:], expert_raw[:], float(E) - 0.5, None, ALU.is_ge))
            table(dve.tensor_scalar(row_fix[:], row[:], -1.0, float(ZROW), ALU.mult, ALU.add))
            table(dve.tensor_tensor(row_fix[:], row_fix[:], unused[:], ALU.mult))
            table(dve.tensor_tensor(tab_row[:], row[:], row_fix[:], ALU.add), then=False)
            table(dve.tensor_copy(tab_expert[:], expert[:]))
            choices = choice[:].rearrange("p t (s o) -> p (t s) o", o=1).broadcast_to([P, T * TOPK, E])
            table(dve.tensor_tensor(of_expert, iota8[:].rearrange("p (o e) -> p o e", o=1)
                                    .broadcast_to([P, T * TOPK, E]), choices, ALU.is_equal))
            table(dve.tensor_tensor(of_expert, of_expert, first_row[:].rearrange("p (o e) -> p o e", o=1)
                                    .broadcast_to([P, T * TOPK, E]), ALU.mult))
            table(dve.tensor_reduce(shift[:], of_expert, AX.X, ALU.add))
            table(dve.tensor_tensor(pos[:].rearrange("p t s -> p (t s)"), pos_x[:].rearrange("p t s -> p (t s)"),
                                    shift[:], ALU.subtract), then=False)
            assert step == TABLE
            dve.wait_ge(wo_hi_done, 1)
            dve.tensor_tensor(wo_lo[:], wo_raw[:], wo_hi[:], ALU.subtract).then_inc(wo_lo_done, 1)

            def block_slot(m, j, steady):
                b, jb, live, past = block_of(m, j, 2, steady)
                if live:
                    e = dve.value_load(tab_expert[0:1, bass.ds(b, 1)], min_val=0, max_val=E - 1)
                    if past(3):
                        dve.wait_ge(yrow_ready, b - 2)
                    for c in range(CH):
                        dve.wait_ge(sig_ready, CH * b + c + 1)
                        if past(1):
                            dve.wait_ge(g_step, GATED * (b - 1) + 3 * (c + 1))
                        dve.scalar_tensor_tensor(
                            out=gated[:, c], in0=hidden_bank[c][:, 0:BR],
                            scalar=b1[:, bass.ds(e, 1), 0, c:c + 1].rearrange("p o n -> p (o n)"),
                            in1=sig[:, c], op0=ALU.add, op1=ALU.mult).then_inc(g_step, 1)
                        dve.wait_ge(g_step, GATED * b + 3 * c + 1)
                        dve.tensor_copy(g_hi[:, jb, c], gated[:, c]).then_inc(g_step, 1)
                        dve.wait_ge(g_step, GATED * b + 3 * c + 2)
                        dve.tensor_tensor(g_lo[:, jb, c], gated[:, c], g_hi[:, jb, c], ALU.subtract).then_inc(g_step, 1)

            block_slots(dve, block_slot)

            def group_slot(m, j, steady):
                g, k, live, past = late_group(m, j, 0, steady)
                if live:
                    for step in range(GT + 3):
                        n = step
                        if n < GT:
                            dve.wait_ge(xr_in[k][n], 16 * (m + 1))
                            dve.wait_ge(gathered[k][n], 32 * (m + 1))
                            if past(2) and n == 0:
                                dve.wait_ge(out_ready, g - 1)
                            dve.scalar_tensor_tensor(out=res3[:, k, n], in0=yg[:, k, n, 0], scalar=comb[:, bass.ds(g * GT + n, 1), 0],
                                                     in1=xr[:, k, n], op0=ALU.mult, op1=ALU.add).then_inc(mixed_first, 1)
                        n = step - 1
                        if 0 <= n < GT:
                            dve.wait_ge(mixed_first, GT * g + n + 1)
                            dve.scalar_tensor_tensor(out=res3[:, k, n], in0=yg[:, k, n, 1], scalar=comb[:, bass.ds(g * GT + n, 1), 1],
                                                     in1=res3[:, k, n], op0=ALU.mult, op1=ALU.add).then_inc(mixed, 1)
                        n = step - 2
                        if 0 <= n < GT:
                            dve.wait_ge(mixed, GT * g + n + 1)
                            if past(1):
                                dve.wait_ge(mv_ready, GT * (g - 1) + n + 1)
                            dve.bn_stats(stats3[:, n], res3[:, k, n]).then_inc(stats_ready, 1)
                        n = step - 3
                        if 0 <= n < GT:
                            dve.wait_ge(stats_ready, GT * g + n + 1)
                            if past(2) and n == 0:
                                dve.wait_ge(rstd3_step, 2 * (g - 1))
                            after_waits(dve)
                            dve.bn_aggr(mv3[:, k, n], stats3[:, n]).then_inc(mv_ready, 1)
                g, k, live, past = late_group(m, j, 1, steady)
                if live:
                    dve.wait_ge(rstd3_step, 2 * (g + 1))
                    if past(2):
                        dve.wait_ge(stored[k], 16 * (m + (j - 1) // 2))
                    for n in range(GT):
                        ins = dve.tensor_scalar(o3[:, k, n], res3[:, k, n], mv3[:, k, n, 0:1], rstd3[:, k, n:n + 1],
                                                ALU.subtract, ALU.mult)
                    ins.then_inc(out_ready, 1)

            group_slots(dve, group_slot)


_CONSTANTS = ("rope", "eye", "before", "ones", "iota8", "base8")


def arrange(inputs):
    g = {k.split("_", 1)[1]: np.asarray(v) for k, v in inputs.items()}
    x = g["attn_x"].reshape(T, P, D)
    wup = g["attn_Wup"].reshape(LAT, H, 2, DH).transpose(0, 2, 1, 3).reshape(LAT, 2 * D)
    bup = g["attn_bup"].reshape(H, 2, DH).transpose(1, 0, 2).reshape(2 * D)

    def rows(a, n):
        return np.broadcast_to(a, (P, n))

    def chunks(a):
        return a.reshape(NC, P, -1).transpose(1, 0, 2)

    d = {
        "x": x,
        "xT": x.reshape(T, P, NC, P).transpose(0, 3, 2, 1),
        "wq": chunks(g["attn_Wq"]),
        "wdown": chunks(g["attn_Wdown"]),
        "bdown": g["attn_bdown"].reshape(LAT, 1),
        "wup": np.concatenate([wup, bup.reshape(1, 2 * D)], 0),
        "bq": g["attn_bq"].reshape(1, D),
        "wout": chunks(g["attn_Wout"]),
        "bout": rows(g["attn_bout"], D),
        "wg": chunks(g["ffn_Wg"].T),
        "w1": g["ffn_W1"].transpose(0, 2, 1).reshape(E, NC, P, 2 * HID).transpose(0, 2, 1, 3).reshape(E, P, NC * 2 * HID),
        "b1": g["ffn_b1"].reshape(E, 2, HID // P, P).transpose(3, 0, 1, 2),
        "wo": g["ffn_Wo"].T.reshape(HID // P, P, D).transpose(1, 0, 2),
        "bo": rows(g["ffn_bo"], D),
    }
    d.update(shape_constants())
    return {k: np.ascontiguousarray(v) for k, v in d.items()}


def kernel(**inputs):
    import concourse.bacc as _bacc
    from concourse.bass_utils import run_bass_kernel_spmd as _run

    nc = _bacc.Bacc("TRN2", target_bir_lowering=False, num_devices=1)
    arrays, args = {}, {}
    for name, a in arrange(inputs).items():
        arrays[f"in_{name}_dram"] = a
        args[name] = nc.dram_tensor(f"in_{name}_dram", a.shape, mybir.dt.from_np(a.dtype), kind="ExternalInput").ap()
    out = nc.dram_tensor("out_0_dram", (N, D), F32, kind="ExternalOutput").ap()
    postln_kernel(nc, args, out)
    r = _run(nc, [arrays], core_ids=[0])
    return r.results[0]["out_0_dram"].reshape(4, 1024, D)
```

```python
from contextlib import ExitStack

import numpy as np

import concourse.bass as bass
from concourse import mybir

F32 = mybir.dt.float32
BF16 = mybir.dt.bfloat16
U32 = mybir.dt.uint32
I32 = mybir.dt.int32
ALU = mybir.AluOpType
ACT = mybir.ActivationFunctionType
AX = mybir.AxisListType

P = 128
N, D = 4096, 256
NC = D // P
H, DH = 16, 16
HG = H * H
LAT = 64
E, HID = 8, 512
TOPK = 2
T = N // P
GT = 4
NG = T // GT
U = 2 * GT
BR = 256
CAP = N + BR
NB = N * TOPK // BR + E - 1
ZROW = E * CAP
ROWS = ZROW + BR
LN_EPS, GATE_EPS = 1e-5, 1e-9
QUARTER = DH ** -0.5

DIMS = (8, 7, 6, 6)
HEADS = (12, 10, 10, 9)
FILL_DIMS = 11
DRAIN_HEADS = 12


def shape_constants():
    inv = (np.float32(1.0) / np.power(np.float32(10000.0), np.arange(0, DH, 2, dtype=np.float32) / np.float32(DH))).astype(np.float32)
    ang = np.arange(1024, dtype=np.float32)[:, None] * inv[None, :]
    cos, sin = np.cos(ang).astype(np.float32), np.sin(ang).astype(np.float32)
    rope = np.stack([np.concatenate([cos, cos], 1), np.concatenate([-sin, sin], 1)], 1)
    rope = rope.reshape(U, P, 2 * DH).transpose(1, 0, 2)
    return {
        "rope": np.ascontiguousarray(rope),
        "eye": np.eye(P, dtype=np.float32),
        "before": np.triu(np.ones((P, P), np.float32), 1),
        "ones": np.ones((P, P), np.float32),
        "iota8": np.ascontiguousarray(np.broadcast_to(np.arange(E, dtype=np.float32), (P, E))),
        "base8": np.ascontiguousarray(np.broadcast_to(np.arange(E, dtype=np.float32) * CAP, (P, E))),
        "iotab": np.ascontiguousarray(np.broadcast_to(np.arange(NB, dtype=np.float32), (P, NB))),
    }


def bc(ap, shape):
    return ap.broadcast_to(shape)


def postln_kernel(nc, d, out):
    with ExitStack() as ctx:
        def sb(name, shape, dt=F32):
            return ctx.enter_context(nc.sbuf_tensor(name, shape, dt))

        def psum(name, shape):
            return ctx.enter_context(nc.psum_tensor(name, shape, F32))

        def sem(name):
            return ctx.enter_context(nc.semaphore(name))

        routed_x = nc.dram_tensor("routed_x", (ROWS, D), F32, kind="Internal").ap()
        x1_dram = nc.dram_tensor("x1_dram", (T, P, D), F32, kind="Internal").ap()
        routed_y = nc.dram_tensor("routed_y", (NB * BR, D), F32, kind="Internal").ap()

        eye = sb("eye", [P, P])
        before = sb("before", [P, P])
        ones = sb("ones_sb", [P, P])
        before_b = sb("before_b", [P, P], BF16)
        ones_b = sb("ones_b", [P, P], BF16)
        iota8 = sb("iota8", [P, E])
        base8 = sb("base8", [P, E])
        rope = sb("rope", [P, U, 2 * DH])
        wq = sb("wq", [P, NC, D])
        wdown = sb("wdown", [P, NC, LAT])
        bdown = sb("bdown", [LAT, 1])
        wup = sb("wup", [LAT + 1, 2 * D])
        bq = sb("bq", [1, D])
        wout = sb("wout", [P, NC, D])
        bout = sb("bout", [1, D])
        wg = sb("wg", [P, NC, E])
        w1_hi = sb("w1_hi", [P, E, NC * 2 * HID], BF16)
        w1_lo = sb("w1_lo", [P, E, NC * 2 * HID], BF16)
        comb = sb("comb", [P, T, TOPK])
        pos_x = sb("pos_x", [P, T, TOPK])
        choice = sb("choice", [P, T, TOPK])
        pos = sb("pos", [P, T, TOPK], U32)
        shift = sb("shift", [P, T * TOPK])
        run = sb("run", [P, E])

        stage1 = ctx.enter_context(ExitStack())

        def sb1(name, shape, dt=F32):
            return stage1.enter_context(nc.sbuf_tensor(name, shape, dt))

        w1_raw = sb1("w1_raw", [P, NC * 2 * HID])
        xt = sb1("xt", [P, GT, NC, P])
        xtok = sb1("xtok", [P, GT, D])
        x1 = sb1("x1", [P, U, D])
        lat = sb1("lat", [LAT + 1, 2, P])
        qk_cos = sb1("qk_cos", [P, 2 * D])
        qk_sin = sb1("qk_sin", [P, 2 * D])
        qkr = sb1("qkr", [P, 2, 2 * D])
        v = sb1("v", [P, GT, D])
        sprod = sb1("sprod", [P, 2, DH, HG])
        smax = sb1("smax", [P, H])
        sdiff = sb1("sdiff", [P, 2, HG])
        eye_neg = sb1("eye_neg", [P, P], BF16)
        probs = sb1("probs", [P, 2, HG])
        zsum = sb1("zsum", [P, H])
        zinv = sb1("zinv", [P, H])
        vprod = sb1("vprod", [P, HG, H])
        osum = sb1("osum", [P, D])
        onorm = sb1("onorm", [P, 2, D])
        ot = sb1("ot", [P, NC, P])
        res = sb1("res", [P, 2, D])
        stats = sb1("stats", [P, 6])
        mv = sb1("mv", [P, 2, 2])
        veps = sb1("veps", [P, 2])
        neg_mean = sb1("neg_mean", [P, 1])
        mean_shift = sb1("mean_shift", [P, 1])
        mhalf = sb1("mhalf", [P, 1])
        rstd = sb1("rstd", [P, 2])
        x1t = sb1("x1t", [P, NC, P])
        gmax = sb1("gmax", [P, GT])
        gdiff = sb1("gdiff", [P, GT, E])
        gexp = sb1("gexp", [P, GT, E])
        gz = sb1("gz", [P, GT])
        gzinv = sb1("gzinv", [P, GT])
        score = sb1("score", [P, GT, E])
        top = sb1("top", [P, GT, 8])
        topi = sb1("topi", [P, GT, 8], U32)
        topf = sb1("topf", [P, GT, TOPK])
        vsum = sb1("vsum", [P, GT])
        vinv = sb1("vinv", [P, GT])
        onehot = sb1("onehot", [P, GT, TOPK, E])
        member = sb1("member", [P, GT, E], BF16)
        pos8 = sb1("pos8", [P, GT, E])
        pos_sel = sb1("pos_sel", [P, GT, TOPK, E])
        posf = sb1("posf", [P, GT, TOPK])
        posi = sb1("posi", [P, 2, GT, TOPK], U32)

        count = sb("count", [P, E])
        count_i = sb("count_i", [P, E], I32)
        blocks_i = sb("blocks_i", [P, E], I32)
        blocks = sb("blocks", [P, E])
        blocks_to = sb("blocks_to", [P, E])
        first_row = sb("first_row", [P, E])
        expert_raw = sb("expert_raw", [P, NB])
        expert = sb("expert", [P, NB])
        row = sb("row", [P, NB])
        unused = sb("unused", [P, NB])
        row_fix = sb("row_fix", [P, NB])
        iotab = sb("iotab", [P, NB])
        tab_expert = sb("tab_expert", [P, NB], I32)
        tab_row = sb("tab_row", [P, NB], I32)
        tab_end = sb("tab_end", [P, E], I32)
        zeros = sb("zeros", [P, BR // P, D])

        CH = HID // P
        b1 = sb("b1", [P, E, 2, CH])
        wo_raw = sb("wo_raw", [P, CH, D])
        wo_hi = sb("wo_hi", [P, CH, D], BF16)
        wo_lo = sb("wo_lo", [P, CH, D], BF16)
        xrow = sb("xrow", [P, 3, BR // P, D])
        eye_b = sb("eye_b", [P, P], BF16)
        xts = sb("xts", [P, 3, 2, NC, BR], BF16)

        pick = sb("pick", [P, 2, GT, TOPK], U32)
        bo = sb("bo", [P, D])
        stats3 = sb("stats3", [P, GT, 6])
        mv3 = sb("mv3", [P, 2, GT, 2])
        veps3 = sb("veps3", [P, GT])
        mhalf3 = sb("mhalf3", [P, GT])
        rstd3 = sb("rstd3", [P, 2, GT])

        sprod_all = sprod[:].rearrange("p b d n -> p (b d n)")
        vprod_all = vprod[:].rearrange("p a g -> p (a g)")
        sig = sprod_all[:, 0:1024].rearrange("p (c n) -> p c n", c=CH)
        gated = sprod_all[:, 1024:2048].rearrange("p (c n) -> p c n", c=CH)
        g_hi = sprod_all[:, 2048:3584].bitcast(BF16).rearrange("p (b c n) -> p b c n", b=3, c=CH)
        g_lo = sprod_all[:, 3584:5120].bitcast(BF16).rearrange("p (b c n) -> p b c n", b=3, c=CH)
        yg = sprod_all[:, 4096:8192].rearrange("p (b t s n) -> p b t s n", b=2, t=GT, s=TOPK)
        yrow = sprod_all[:, 5120:6656].rearrange("p (b r n) -> p b r n", b=3, r=BR // P)
        xr = x1[:].rearrange("p (b t) n -> p b t n", b=2)
        xsplit = w1_raw[:, 0:1536].bitcast(BF16).rearrange("p (b s n) -> p b s n", b=3, s=2)
        passed = vprod_all[:, 0:NB * E].rearrange("p (b e) -> p b e", e=E)
        is_expert = vprod_all[:, 512:512 + NB * E].rearrange("p (b e) -> p b e", e=E)
        of_expert = vprod_all[:, 1024:1024 + T * TOPK * E].rearrange("p (k e) -> p k e", e=E)
        res3 = vprod_all[:, 0:2048].rearrange("p (b t n) -> p b t n", b=2, t=GT)
        o3 = vprod_all[:, 2048:4096].rearrange("p (b t n) -> p b t n", b=2, t=GT)

        ps_qk = psum("ps_qk", [P, 512])
        ps_v = psum("ps_v", [P, 512])
        ps_s = psum("ps_s", [P, 512])
        ps_t = psum("ps_t", [P, 512])
        ps_o = psum("ps_o", [P, 512])
        ps_y = psum("ps_y", [P, 512])
        ps_g = psum("ps_g", [P, 512])
        ps_r = psum("ps_r", [P, 512])
        ps_lat = ps_v[0:LAT, D:D + P]
        ps_xt = ps_o[:].bitcast(BF16)
        logits = ps_g[:, 0:GT * E].rearrange("p (t e) -> p t e", e=E)
        ps_pos = ps_r[:, 0:GT * E].rearrange("p (t e) -> p t e", e=E)
        ps_tot = ps_r[:, GT * E:(GT + 1) * E]

        w_in, wq_in, rope_in, before_in = sem("w_in"), sem("wq_in"), sem("rope_in"), sem("before_in")
        x_in = [sem(f"x_in{k}") for k in range(GT)]
        xt_in = [sem(f"xt_in{k}") for k in range(GT)]
        w1_in = sem("w1_in")
        lat_ready, lat_copied = sem("lat_ready"), sem("lat_copied")
        qkv_ready, qk_taken = sem("qkv_ready"), sem("qk_taken")
        rope_step = sem("rope_step")
        sprod_dve, sprod_pool = sem("sprod_dve"), sem("sprod_pool")
        scores_ready, scores_copied = sem("scores_ready"), sem("scores_copied")
        max_ready, diff_ready = sem("max_ready"), sem("diff_ready")
        exp_ready = sem("exp_ready")
        vprod_dve, vprod_pool = sem("vprod_dve"), sem("vprod_pool")
        norm_step = sem("norm_step")
        ot_ready, ot_copied = sem("ot_ready"), sem("ot_copied")
        y_ready, ln_step = sem("y_ready"), sem("ln_step")
        rstd_ready, x1_ready = sem("rstd_ready"), sem("x1_ready")
        v_copied, lat_ones, count_consts, consts_in = sem("v_copied"), sem("lat_ones"), sem("count_consts"), sem("consts_in")
        x1t_ready, x1t_copied, x1_stored = sem("x1t_ready"), sem("x1t_copied"), sem("x1_stored")
        logits_ready, gexp_ready, route_step = sem("logits_ready"), sem("gexp_ready"), sem("route_step")
        count_ready = sem("count_ready")
        w1_hi_done, w1_left, w1_lo_done = sem("w1_hi_done"), sem("w1_left"), sem("w1_lo_done")
        eye_neg_set, shift_step = sem("eye_neg_set"), sem("shift_step")
        const_set = sem("const_set")
        scattered, pos_kept = sem("scattered"), sem("pos_kept")
        stored = [sem(f"stored{k}") for k in range(2)]
        waits_met = sem("waits_met")
        w2_in = sem("w2_in")
        table_step, zeros_set, tails_zeroed = sem("table_step"), sem("zeros_set"), sem("tails_zeroed")
        wo_hi_done, wo_lo_done = sem("wo_hi_done"), sem("wo_lo_done")
        xrow_in = [sem(f"xrow_in{k}") for k in range(3)]
        x_hi_done, x_lo_done = sem("x_hi_done"), sem("x_lo_done")
        xrow_t, xt_copied, eye_b_set = sem("xrow_t"), sem("xt_copied"), sem("eye_b_set")
        hidden_ready, sig_ready, g_step = sem("hidden_ready"), sem("sig_ready"), sem("g_step")
        yrow_ready, yrow_copied, yrow_biased = sem("yrow_ready"), sem("yrow_copied"), sem("yrow_biased")
        yrow_out = [sem(f"yrow_out{k}") for k in range(3)]
        picked = sem("picked")
        gathered = [[sem(f"gathered{k}{n}") for n in range(GT)] for k in range(2)]
        xr_in = [[sem(f"xr_in{k}{n}") for n in range(GT)] for k in range(2)]
        mixed_first, mixed = sem("mixed_first"), sem("mixed")
        stats_ready, mv_ready = sem("stats_ready"), sem("mv_ready")
        veps3_ready, rstd3_ready, out_ready = sem("veps3_ready"), sem("rstd3_ready"), sem("out_ready")

        ROPE, NORM, LN, ROUTE = 3, 4, 4, 25
        WEIGHT_LOADS = 4
        W1C = NC * 2 * HID // 512
        CONST_LOADS = 7
        LATE_LOADS = 4
        TABLE = 24
        GATED = 3 * CH
        hidden_bank = [ps_qk, ps_v, ps_s, ps_t]

        block = ctx.enter_context(nc.Block())

        def after_waits(eng):
            eng.sem_inc(waits_met, 1)

        def slots(eng, slot):
            for j in range(U):
                slot(0, j, False)
            with eng.Fori(1, T // U) as m:
                for j in range(U):
                    slot(m, j, True)
            for j in range(U):
                slot(T // U, j, False)

        def tile_of(m, j, lag, steady):
            lag += 2
            t = m * U + (j - lag)
            return t, (j - lag) % U, steady or 0 <= t < T, (lambda k: steady or t >= k)

        def weight_chunks(m, j, steady):
            if j % GT == GT - 1:
                g, first = m * 2 + j // GT, 0
            elif j % GT == 0:
                g, first = m * 2 + j // GT - 1, 2
            else:
                return []
            return [(g, first), (g, first + 1)] if steady or 0 <= g < E else []

        def dve_dims(m, j, steady):
            return FILL_DIMS if not steady and m == 0 and j < GT else DIMS[j % GT]

        def dve_heads(m, j, steady):
            return DRAIN_HEADS if not steady and m == T // U else HEADS[j % GT]

        def rounds(m, j, lag):
            return m * 2 + (j - lag - 2) // GT + 1

        def group_of(m, j, steady):
            q = m * 2 + (j - 11) // GT
            return q, ((j - 11) // GT) % 2, j % GT == 3 and (steady or 0 <= q < NG), (lambda k: steady or q >= k)

        def block_slots(eng, slot):
            for m in range(2):
                for j in range(3):
                    slot(m, j, False)
            with eng.Fori(2, NB // 3) as m:
                for j in range(3):
                    slot(m, j, True)
            for j in range(3):
                slot(NB // 3, j, False)

        def block_of(m, j, lag, steady):
            t = m * 3 + (j - lag)
            return t, (j - lag) % 3, steady or 0 <= t < NB, (lambda k: steady or t >= k)

        def group_slots(eng, slot):
            for m in range(2):
                for j in range(2):
                    slot(m, j, False)
            with eng.Fori(2, NG // 2) as m:
                for j in range(2):
                    slot(m, j, True)
            slot(NG // 2, 0, False)

        def late_group(m, j, lag, steady):
            g = m * 2 + (j - lag)
            return g, (j - lag) % 2, steady or 0 <= g < NG, (lambda k: steady or g >= k)

        @block.sync
        def _(sp):
            for name, buf in (("wdown", wdown), ("bdown", bdown), ("wup", wup), ("bq", bq)):
                sp.dma_start(buf[:], d[name]).then_inc(w_in, 16)
            sp.dma_start(rope[:], d["rope"]).then_inc(rope_in, 16)
            sp.dma_start(xt[:, 1], d["xT"][1]).then_inc(xt_in[1], 16)
            for name, buf in (("eye", eye), ("wout", wout), ("bout", bout), ("wg", wg), ("iota8", iota8),
                              ("base8", base8), ("base8", run)):
                sp.dma_start(buf[:], d[name]).then_inc(consts_in, 16)
                if name == "eye":
                    for t in range(2, GT):
                        sp.dma_start(xt[:, t], d["xT"][t]).then_inc(xt_in[t], 16)

            def slot(m, j, steady):
                t, jt, live, past = tile_of(m, j, 0, steady)
                if live:
                    if past(GT):
                        sp.wait_ge(ln_step, LN * (t - GT) + 1)
                    sp.dma_start(xtok[:, jt % GT], d["x"][t]).then_inc(x_in[jt % GT], 16)
                t, jt, live, past = tile_of(m, j, -2, steady)
                if live and past(GT):
                    sp.wait_ge(qkv_ready, t - GT + 1)
                    sp.dma_start(xt[:, jt % GT], d["xT"][t]).then_inc(xt_in[jt % GT], 16)
                t, jt, live, past = tile_of(m, j, 4, steady)
                if live:
                    sp.wait_ge(x1_ready, t + 1)
                    sp.dma_start(x1_dram[t], x1[:, jt]).then_inc(x1_stored, 16)
                    sp.wait_ge(x1_stored, 16 * (t + 1))
                    after_waits(sp)
                if j % GT == 1 and (steady or m * 2 + j // GT < E):
                    g = m * 2 + j // GT
                    if steady or g > 0:
                        sp.wait_ge(w1_lo_done, W1C * g)
                    sp.dma_start(w1_raw[:], d["w1"][g]).then_inc(w1_in, 16)
                if not steady and m == 0 and j == GT:
                    for name, buf in (("b1", b1), ("wo", wo_raw), ("bo", bo), ("iotab", iotab)):
                        sp.dma_start(buf[:], d[name]).then_inc(w2_in, 16)

            slots(sp, slot)
            sp.wait_ge(zeros_set, 1)
            sp.dma_start(routed_x[ZROW:ZROW + BR].rearrange("(r p) d -> p r d", p=P), zeros[:]).then_inc(tails_zeroed, 16)
            sp.wait_ge(table_step, 1)
            for e in range(E):
                end = sp.value_load(tab_end[0:1, e:e + 1], min_val=e * CAP, max_val=e * CAP + N)
                sp.dma_start(routed_x[bass.ds(end, BR)].rearrange("(r p) d -> p r d", p=P),
                             zeros[:]).then_inc(tails_zeroed, 16)
            sp.wait_ge(tails_zeroed, 16 * (E + 1))
            sp.wait_ge(scattered, 16 + 16 * T * TOPK)
            sp.wait_ge(table_step, TABLE)

            def block_slot(m, j, steady):
                b, jb, live, past = block_of(m, j, 0, steady)
                if live:
                    if past(3):
                        sp.wait_ge(x_lo_done, b - 2)
                    src = sp.value_load(tab_row[0:1, bass.ds(b, 1)], min_val=0, max_val=ROWS - BR)
                    sp.dma_start(xrow[:, jb], routed_x[bass.ds(src, BR)].rearrange("(r p) d -> p r d", p=P)
                                 ).then_inc(xrow_in[jb], 16)
                b, jb, live, past = block_of(m, j, 3, steady)
                if live:
                    sp.wait_ge(yrow_biased, b + 1)
                    sp.dma_start(routed_y.rearrange("(b r p) d -> b p r d", p=P, r=BR // P)[b], yrow[:, jb]
                                 ).then_inc(yrow_out[jb], 16)

            block_slots(sp, block_slot)

            def group_slot(m, j, steady):
                g, k, live, past = late_group(m, j, 0, steady)
                if live:
                    for n in range(GT):
                        if past(2):
                            sp.wait_ge(mixed_first, GT * (g - 2) + n + 1)
                        sp.dma_start(xr[:, k, n], x1_dram[g * GT + n]).then_inc(xr_in[k][n], 16)

            group_slots(sp, group_slot)
            for k in range(2):
                sp.wait_ge(stored[k], 16 * NG // 2)

        @block.tensor
        def _(pe):
            def latent(m, j, t, jt, past):
                pe.wait_ge(xt_in[jt % GT], 16 * rounds(m, j, -2))
                if past(1):
                    pe.wait_ge(lat_copied, t)
                if past(2):
                    pe.wait_ge(v_copied, t - 1)
                for c in range(NC):
                    mm = pe.matmul(ps_lat, wdown[:, c], xt[:, jt % GT, c], start=(c == 0), stop=(c == NC - 1))
                mm.then_inc(lat_ready, 1)

            def qkv(t, jt, past):
                pe.wait_ge(lat_copied, t + 1)
                if past(1):
                    pe.wait_ge(qk_taken, t)
                for c in range(NC):
                    pe.matmul(ps_qk[:, 0:D], xt[:, jt % GT, c], wq[:, c], start=(c == 0), stop=False)
                pe.matmul(ps_qk[:, 0:D], ones[0:1, :], bq[:], start=False, stop=True)
                pe.matmul(ps_qk[:, D:2 * D], lat[:, jt % 2], wup[:, 0:D], start=True, stop=True)
                pe.matmul(ps_v[:, 0:D], lat[:, jt % 2], wup[:, D:2 * D], start=True, stop=True).then_inc(qkv_ready, 1)

            pe.wait_ge(w_in, 16 * WEIGHT_LOADS)
            pe.wait_ge(wq_in, 16)
            pe.wait_ge(count_consts, 2)
            pe.wait_ge(lat_ones, 1)

            def weights_left(g, c):
                pe.wait_ge(w1_hi_done, g + 1)
                if c > 0 or not isinstance(g, int) or g > 0:
                    pe.wait_ge(w1_lo_done, g * W1C + c)
                at = c * 512
                pe.matmul(ps_o[:], eye[:], w1_raw[:, at:at + 512], start=True, stop=False)
                pe.matmul(ps_o[:], eye_neg[:], w1_hi[:, bass.ds(g, 1), at:at + 512].rearrange("p o n -> p (o n)"),
                          start=False, stop=True).then_inc(w1_left, 1)

            def slot(m, j, steady):
                if not steady and m == 0 and j == 3:
                    pe.wait_ge(consts_in, 16 * CONST_LOADS)
                    pe.wait_ge(eye_neg_set, 1)
                for g, c in weight_chunks(m, j, steady)[:1]:
                    weights_left(g, c)
                t, jt, live, past = tile_of(m, j, 1, steady)
                if live:
                    b = jt % 2
                    pe.wait_ge(sprod_dve, t + 1)
                    pe.wait_ge(sprod_pool, t + 1)
                    if past(1):
                        pe.wait_ge(scores_copied, t)
                    for k in range(DH):
                        mm = pe.matmul(ps_s[:, 0:HG], eye[:], sprod[:, b, k], start=(k == 0), stop=(k == DH - 1))
                    mm.then_inc(scores_ready, 1)
                t, jt, live, past = tile_of(m, j, 3, steady)
                if live:
                    pe.wait_ge(norm_step, NORM * (t + 1))
                    if past(1):
                        pe.wait_ge(ot_copied, t)
                    if past(3):
                        pe.wait_ge(x1t_copied, t - 2)
                    for c in range(NC):
                        tr = pe.transpose(ps_t[:, c * P:(c + 1) * P], onorm[:, jt % 2, c * P:(c + 1) * P], eye[:])
                    tr.then_inc(ot_ready, 1)
                t, jt, live, past = tile_of(m, j, 5, steady)
                if live:
                    pe.wait_ge(x1_ready, t + 1)
                    if past(1):
                        pe.wait_ge(x1t_copied, t)
                    if not steady:
                        pe.wait_ge(ot_copied, min(t + 2, T))
                    for c in range(NC):
                        tr = pe.transpose(ps_t[:, D + c * P:D + (c + 1) * P], x1[:, jt, c * P:(c + 1) * P], eye[:])
                    tr.then_inc(x1t_ready, 1)
                t, jt, live, past = tile_of(m, j, -2, steady)
                if live:
                    latent(m, j, t, jt, past)
                t, jt, live, past = tile_of(m, j, 3, steady)
                if live:
                    pe.wait_ge(ot_copied, t + 1)
                    if past(1):
                        pe.wait_ge(ln_step, LN * (t - 1) + 1)
                    for c in range(NC):
                        pe.matmul(ps_y[:, 0:D], ot[:, c], wout[:, c], start=(c == 0), stop=False)
                    mm = pe.matmul(ps_y[:, 0:D], ones[0:1, :], bout[:], start=False, stop=True)
                    mm.then_inc(y_ready, 1)
                t, jt, live, past = tile_of(m, j, -1, steady)
                if live:
                    qkv(t, jt, past)
                q, k, live, past = group_of(m, j, steady)
                if live:
                    pe.wait_ge(route_step, ROUTE * q + 19)
                    for k in range(GT):
                        for kk in range(k):
                            pe.matmul(ps_pos[:, k], ones_b[:], member[:, kk], start=(kk == 0), stop=False)
                        pe.matmul(ps_pos[:, k], before_b[:], member[:, k], start=(k == 0), stop=True)
                    for k in range(GT):
                        mm = pe.matmul(ps_tot, ones_b[:], member[:, k], start=(k == 0), stop=(k == GT - 1))
                    mm.then_inc(count_ready, 1)
                for g, c in weight_chunks(m, j, steady)[1:]:
                    weights_left(g, c)
                t, jt, live, past = tile_of(m, j, 5, steady)
                if live:
                    pe.wait_ge(x1t_copied, t + 1)
                    if jt % GT == 0 and past(GT):
                        pe.wait_ge(route_step, ROUTE * (rounds(m, j, 5) - 2) + 2)
                    for c in range(NC):
                        mm = pe.matmul(logits[:, jt % GT], x1t[:, c], wg[:, c], start=(c == 0), stop=(c == NC - 1))
                    mm.then_inc(logits_ready, 1)

            slots(pe, slot)
            pe.wait_ge(w1_lo_done, W1C * E)
            pe.wait_ge(wo_hi_done, 1)
            pe.wait_ge(wo_lo_done, 1)
            pe.wait_ge(eye_b_set, 1)
            pe.wait_ge(table_step, TABLE)
            pe.wait_ge(gexp_ready, NG)

            def block_slot(m, j, steady):
                b, jb, live, past = block_of(m, j, 2, steady)
                if live:
                    e = pe.value_load(tab_expert[0:1, bass.ds(b, 1)], min_val=0, max_val=E - 1)
                    pe.wait_ge(xt_copied, b + 1)
                    for c in range(CH):
                        if past(1):
                            pe.wait_ge(g_step, GATED * (b - 1) + 3 * c + 1)
                        for half in range(2):
                            n = 0
                            for w, x in ((w1_hi, 0), (w1_hi, 1), (w1_lo, 0)):
                                for kc in range(NC):
                                    at = kc * 2 * HID + half * HID + c * P
                                    mm = pe.matmul(hidden_bank[c][:, half * BR:(half + 1) * BR],
                                                   w[:, bass.ds(e, 1), at:at + P].rearrange("p o n -> p (o n)"), xts[:, jb, x, kc],
                                                   start=(n == 0), stop=(n == 5))
                                    n += 1
                        mm.then_inc(hidden_ready, 1)
                b, jb, live, past = block_of(m, j, 1, steady)
                if live:
                    pe.wait_ge(x_hi_done, b + 1)
                    pe.wait_ge(x_lo_done, b + 1)
                    if past(1):
                        pe.wait_ge(xt_copied, b)
                    for s in range(2):
                        for r in range(BR // P):
                            for c in range(NC):
                                at = (s * NC + c) * BR + r * P
                                tr = pe.transpose(ps_xt[:, at:at + P], xsplit[:, jb, s, r * D + c * P:r * D + (c + 1) * P],
                                                  eye_b[:])
                    tr.then_inc(xrow_t, 1)
                b, jb, live, past = block_of(m, j, 3, steady)
                if live:
                    if past(1):
                        pe.wait_ge(yrow_copied, b)
                    pe.wait_ge(g_step, GATED * (b + 1))
                    for r in range(BR // P):
                        n = 0
                        for c in range(CH):
                            for gg, w in ((g_hi, wo_hi), (g_lo, wo_hi), (g_hi, wo_lo)):
                                mm = pe.matmul(ps_y[:, r * D:(r + 1) * D], gg[:, jb, c, r * P:(r + 1) * P], w[:, c],
                                               start=(n == 0), stop=(n == 3 * CH - 1))
                                n += 1
                    mm.then_inc(yrow_ready, 1)

            block_slots(pe, block_slot)

        @block.scalar
        def _(act):
            act.dma_start(xt[:, 0], d["xT"][0]).then_inc(xt_in[0], 16)
            act.dma_start(wq[:], d["wq"]).then_inc(wq_in, 16)
            act.wait_ge(w_in, 16 * WEIGHT_LOADS)

            def copy_latent(t, jt, past):
                act.wait_ge(lat_ready, t + 1)
                if past(2):
                    act.wait_ge(qkv_ready, t - 1)
                act.activation(lat[0:LAT, jt % 2], ps_lat, ACT.Identity, bias=bdown[:]).then_inc(lat_copied, 1)

            def copy_weights_left(g, c):
                act.wait_ge(w1_left, g * W1C + c + 1)
                act.copy(w1_lo[:, bass.ds(g, 1), c * 512:(c + 1) * 512].rearrange("p o n -> p (o n)"), ps_o[:]).then_inc(w1_lo_done, 1)

            def slot(m, j, steady):
                if not steady and m == 0 and j == 3:
                    act.wait_ge(consts_in, 16 * CONST_LOADS)
                    act.activation(eye_neg[:], eye[:], ACT.Copy, scale=-1.0).then_inc(eye_neg_set, 1)
                t, jt, live, past = tile_of(m, j, 4, steady)
                if live:
                    act.wait_ge(rstd_ready, t + 1)
                    if past(1):
                        act.wait_ge(x1_ready, t)
                    inverse = rstd[:, jt % 2:jt % 2 + 1]
                    act.activation(neg_mean[:], mv[:, jt % 2, 0:1], ACT.Copy, scale=-1.0).then_inc(shift_step, 1)
                    act.wait_ge(shift_step, 2 * t + 1)
                    act.activation(mean_shift[:], neg_mean[:], ACT.Copy, scale=inverse).then_inc(shift_step, 1)
                    act.wait_ge(shift_step, 2 * t + 2)
                    act.activation(x1[:, jt], res[:, jt % 2], ACT.Identity, bias=mean_shift[:],
                                   scale=inverse).then_inc(x1_ready, 1)
                for g, c in weight_chunks(m, j, steady)[:1]:
                    copy_weights_left(g, c)
                q, k, live, past = group_of(m, j, steady)
                if live:
                    act.wait_ge(route_step, ROUTE * q + 2)
                    act.activation(gexp[:], gdiff[:], ACT.Exp).then_inc(gexp_ready, 1)
                t, jt, live, past = tile_of(m, j, 1, steady)
                if live:
                    act.wait_ge(scores_ready, t + 1)
                    if past(2):
                        act.wait_ge(exp_ready, t - 1)
                    act.copy(sdiff[:, jt % 2], ps_s[:, 0:HG]).then_inc(scores_copied, 1)
                t, jt, live, past = tile_of(m, j, 3, steady)
                if live:
                    act.wait_ge(ot_ready, t + 1)
                    if past(2):
                        act.wait_ge(x1t_ready, t - 1)
                    if past(1):
                        act.wait_ge(y_ready, t)
                    act.copy(ot[:].rearrange("p c k -> p (c k)"), ps_t[:, 0:D]).then_inc(ot_copied, 1)
                t, jt, live, past = tile_of(m, j, 5, steady)
                if live:
                    act.wait_ge(x1t_ready, t + 1)
                    if past(1):
                        act.wait_ge(logits_ready, t)
                    act.copy(x1t[:].rearrange("p c k -> p (c k)"), ps_t[:, D:2 * D]).then_inc(x1t_copied, 1)
                if j % GT == 2 and (steady or m * 2 + j // GT < NG):
                    g = m * 2 + j // GT
                    act.wait_ge(w1_in, 16 * (g + 1))
                    act.copy(w1_hi[:, g], w1_raw[:]).then_inc(w1_hi_done, 1)
                t, jt, live, past = tile_of(m, j, -2, steady)
                if live:
                    if past(1):
                        act.wait_ge(qkv_ready, t)
                    copy_latent(t, jt, past)
                t, jt, live, past = tile_of(m, j, -1, steady)
                if live:
                    act.wait_ge(qkv_ready, t + 1)
                    if past(GT):
                        act.wait_ge(vprod_dve, t - GT + 1)
                        act.wait_ge(vprod_pool, t - GT + 1)
                    act.copy(v[:, jt % GT], ps_v[:, 0:D]).then_inc(v_copied, 1)
                for g, c in weight_chunks(m, j, steady)[1:]:
                    copy_weights_left(g, c)
                t, jt, live, past = tile_of(m, j, 1, steady)
                if live:
                    act.wait_ge(diff_ready, t + 1)
                    if past(2):
                        act.wait_ge(norm_step, NORM * (t - 1))
                        act.wait_ge(vprod_pool, t - 1)
                    act.activation(probs[:, jt % 2], sdiff[:, jt % 2], ACT.Exp, scale=QUARTER).then_inc(exp_ready, 1)

            slots(act, slot)
            act.wait_ge(w2_in, 16 * LATE_LOADS)
            act.copy(wo_hi[:], wo_raw[:]).then_inc(wo_hi_done, 1)
            act.copy(eye_b[:], eye[:]).then_inc(eye_b_set, 1)
            act.wait_ge(table_step, TABLE)

            def block_slot(m, j, steady):
                b, jb, live, past = block_of(m, j, 1, steady)
                if live:
                    act.wait_ge(xrow_in[jb], 16 * (m + (j - 1) // 3 + 1))
                    if past(3):
                        act.wait_ge(xrow_t, b - 2)
                    act.copy(xsplit[:, jb, 0], xrow[:, jb].rearrange("p r n -> p (r n)")).then_inc(x_hi_done, 1)
                b, jb, live, past = block_of(m, j, 2, steady)
                if live:
                    e = act.value_load(tab_expert[0:1, bass.ds(b, 1)], min_val=0, max_val=E - 1)
                    for c in range(CH):
                        act.wait_ge(hidden_ready, CH * b + c + 1)
                        if past(1):
                            act.wait_ge(g_step, GATED * (b - 1) + 3 * c + 1)
                        act.activation(sig[:, c], hidden_bank[c][:, BR:2 * BR], ACT.Sigmoid,
                                       bias=b1[:, bass.ds(e, 1), 1, c:c + 1].rearrange("p o n -> p (o n)")).then_inc(sig_ready, 1)
                b, jb, live, past = block_of(m, j, 1, steady)
                if live:
                    act.wait_ge(xrow_t, b + 1)
                    if past(3):
                        act.wait_ge(hidden_ready, CH * (b - 2))
                    act.copy(xts[:, jb].rearrange("p s c n -> p (s c n)"), ps_xt).then_inc(xt_copied, 1)
                b, jb, live, past = block_of(m, j, 3, steady)
                if live:
                    act.wait_ge(yrow_ready, b + 1)
                    if past(3):
                        act.wait_ge(yrow_out[jb], 16 * (m + (j - 3) // 3))
                    act.copy(yrow[:, jb].rearrange("p r n -> p (r n)"), ps_y[:]).then_inc(yrow_copied, 1)

            block_slots(act, block_slot)

            def group_slot(m, j, steady):
                g, k, live, past = late_group(m, j, 1, steady)
                if live:
                    act.wait_ge(out_ready, g + 1)
                    act.dma_start(out.rearrange("(g n p) d -> g p n d", p=P, n=GT)[g], o3[:, k]).then_inc(stored[k], 16)

            act.wait_ge(table_step, TABLE)
            group_slots(act, group_slot)

        @block.gpsimd
        def _(pool):
            pool.dma_start(before[:], d["before"]).then_inc(before_in, 16)
            pool.dma_start(ones[:], d["ones"]).then_inc(scattered, 16)
            pool.memset(mhalf[:], -0.5).then_inc(const_set, 1)
            pool.wait_ge(const_set, 1)
            pool.memset(lat[LAT:LAT + 1], 1.0).then_inc(lat_ones, 1)
            pool.wait_ge(lat_ones, 1)
            pool.wait_ge(before_in, 16)
            pool.wait_ge(scattered, 16)
            pool.tensor_copy(before_b[:], before[:]).then_inc(count_consts, 1)
            pool.tensor_copy(ones_b[:], ones[:]).then_inc(count_consts, 1)
            copies = [(n, s) for n in range(GT) for s in range(TOPK)]
            EARLY = 5

            def scatter(k, n, s):
                pool.indirect_dma_start(routed_x, bass.IndirectOffsetOnAxis(ap=posi[:, k, n, s:s + 1], axis=0),
                                        x1[:, k * GT + n], None).then_inc(scattered, 16)

            def slot(m, j, steady):
                if j % GT == 1 and (steady or 0 <= m * 2 + (j - 13) // GT < NG):
                    pool.wait_ge(scattered, 16 + 16 * GT * TOPK * (m * 2 + (j - 13) // GT + 1))
                t, jt, live, past = tile_of(m, j, 2, steady)
                if live:
                    b = jt % 2
                    pool.wait_ge(exp_ready, t + 1)
                    pool.wait_ge(v_copied, t + 1)
                    if past(1):
                        pool.wait_ge(norm_step, NORM * (t - 1) + 3)
                    first = dve_heads(m, j, steady)
                    n = H - first
                    pool.tensor_tensor(
                        vprod[:, first * DH:].rearrange("p (h d) g -> p h d g", h=n),
                        probs[:, b, first * H:].rearrange("p (h o g) -> p h o g", h=n, o=1).broadcast_to([P, n, DH, H]),
                        v[:, jt % GT].rearrange("p (o g d) -> p o d g", o=1, g=H).broadcast_to([P, n, DH, H]),
                        ALU.mult).then_inc(vprod_pool, 1)
                t, jt, live, past = tile_of(m, j, 0, steady)
                if live:
                    b = jt % 2
                    pool.wait_ge(rope_step, ROPE * (t + 1))
                    if past(2):
                        pool.wait_ge(scores_ready, t - 1)
                    first = dve_dims(m, j, steady)
                    n = DH - first
                    qr = qkr[:, b, 0:D].rearrange("p (h o d) -> p d h o", h=H, o=1)[:, first:].broadcast_to([P, n, H, H])
                    kr = qkr[:, b, D:2 * D].rearrange("p (o g d) -> p d o g", o=1, g=H)[:, first:].broadcast_to([P, n, H, H])
                    pool.tensor_tensor(sprod[:, b, first:].rearrange("p d (h g) -> p d h g", h=H), qr, kr,
                                       ALU.mult).then_inc(sprod_pool, 1)
                t, jt, live, past = tile_of(m, j, 1, steady)
                if live:
                    pool.wait_ge(max_ready, t + 1)
                    diff = sdiff[:, jt % 2].rearrange("p (h g) -> p h g", h=H)
                    pool.tensor_tensor(diff, diff,
                                       smax[:].rearrange("p (h o) -> p h o", o=1).broadcast_to([P, H, H]),
                                       ALU.subtract).then_inc(diff_ready, 1)
                q, k, routed, past = group_of(m, j, steady)
                if routed:
                    pool.wait_ge(route_step, ROUTE * (q + 1))
                    after_waits(pool)
                    for n, s in copies[:EARLY]:
                        scatter(k, n, s)
                t, jt, live, past = tile_of(m, j, 3, steady)
                if live:
                    b = jt % 2
                    pool.wait_ge(ln_step, LN * (t + 1))
                    if past(2):
                        pool.wait_ge(x1_ready, t - 1)
                    pool.tensor_tensor(rstd[:, b:b + 1], veps[:, b:b + 1], mhalf[:], ALU.pow).then_inc(rstd_ready, 1)
                if routed:
                    for n, s in copies[EARLY:]:
                        scatter(k, n, s)

            slots(pool, slot)
            pool.memset(mhalf3[:], -0.5).then_inc(const_set, 1)
            pool.wait_ge(const_set, 2)
            pool.wait_ge(w2_in, 16 * LATE_LOADS)
            pool.wait_ge(table_step, TABLE)

            def block_slot(m, j, steady):
                b, jb, live, past = block_of(m, j, 1, steady)
                if live:
                    pool.wait_ge(x_hi_done, b + 1)
                    if past(3):
                        pool.wait_ge(xrow_t, b - 2)
                    pool.tensor_tensor(xsplit[:, jb, 1], xrow[:, jb].rearrange("p r n -> p (r n)"),
                                       xsplit[:, jb, 0], ALU.subtract).then_inc(x_lo_done, 1)
                b, jb, live, past = block_of(m, j, 3, steady)
                if live:
                    pool.wait_ge(yrow_copied, b + 1)
                    pool.tensor_tensor(yrow[:, jb], yrow[:, jb],
                                       bo[:].rearrange("p (o n) -> p o n", o=1).broadcast_to([P, BR // P, D]),
                                       ALU.add).then_inc(yrow_biased, 1)

            block_slots(pool, block_slot)
            for k in range(3):
                pool.wait_ge(yrow_out[k], 16 * (NB // 3))

            def group_slot(m, j, steady):
                g, k, live, past = late_group(m, j, 0, steady)
                if live:
                    if past(2):
                        for n in range(GT):
                            pool.wait_ge(gathered[k][n], 32 * m)
                    pool.tensor_copy(pick[:, k], pos[:, bass.ds(g * GT, GT)]).then_inc(picked, 1)
                    pool.wait_ge(picked, g + 1)
                    for n in range(GT):
                        if past(2):
                            pool.wait_ge(mixed, GT * (g - 2) + n + 1)
                        after_waits(pool)
                        for s in range(TOPK):
                            pool.indirect_dma_start(
                                yg[:, k, n, s], None, routed_y,
                                bass.IndirectOffsetOnAxis(ap=pick[:, k, n, s:s + 1], axis=0)).then_inc(gathered[k][n], 16)
                g, k, live, past = late_group(m, j, 1, steady)
                if live:
                    pool.wait_ge(veps3_ready, g + 1)
                    if past(2):
                        pool.wait_ge(out_ready, g - 1)
                    pool.tensor_tensor(rstd3[:, k], veps3[:], mhalf3[:], ALU.pow).then_inc(rstd3_ready, 1)

            group_slots(pool, group_slot)

        @block.vector
        def _(dve):
            dve.memset(zeros[:], 0.0).then_inc(zeros_set, 1)
            dve.wait_ge(rope_in, 16)

            def slot(m, j, steady):
                if not steady and m == 0 and j == 4:
                    dve.wait_ge(consts_in, 16 * CONST_LOADS)
                t, jt, live, past = tile_of(m, j, 0, steady)
                t1, jt1, live1, past1 = tile_of(m, j, 1, steady)
                t2, jt2, live2, past2 = tile_of(m, j, 2, steady)
                t3, jt3, live3, past3 = tile_of(m, j, 3, steady)
                b, b1, b2, b3 = jt % 2, jt1 % 2, jt2 % 2, jt3 % 2
                q, k, routed, _ = group_of(m, j, steady)
                at = ROUTE * q
                dims, heads = dve_dims(m, j, steady), dve_heads(m, j, steady)

                if routed:
                    dve.wait_ge(logits_ready, GT * (q + 1))
                    dve.tensor_reduce(gmax[:], logits[:], AX.X, ALU.max).then_inc(route_step, 1)
                if live:
                    dve.wait_ge(qkv_ready, t + 1)
                    if past(1):
                        dve.wait_ge(rope_step, ROPE * t)
                    qk = ps_qk[:].rearrange("p (h d) -> p h d", h=2 * H)
                    dve.tensor_tensor(
                        qk_cos[:].rearrange("p (h d) -> p h d", h=2 * H), qk,
                        rope[:, jt, 0:DH].rearrange("p (o d) -> p o d", o=1).broadcast_to([P, 2 * H, DH]),
                        ALU.mult).then_inc(rope_step, 1)
                if routed:
                    dve.wait_ge(route_step, at + 1)
                    dve.tensor_tensor(gdiff[:], logits[:], gmax[:].rearrange("p (t o) -> p t o", o=1).broadcast_to([P, GT, E]),
                                      ALU.subtract).then_inc(route_step, 1)
                if live:
                    for half in range(2):
                        a, z = half * DH // 2, (1 - half) * DH // 2
                        ins = dve.tensor_tensor(
                            qk_sin[:].rearrange("p (h d) -> p h d", h=2 * H)[:, :, a:a + DH // 2],
                            qk[:, :, z:z + DH // 2],
                            rope[:, jt, DH + a:DH + a + DH // 2].rearrange("p (o d) -> p o d", o=1)
                            .broadcast_to([P, 2 * H, DH // 2]), ALU.mult)
                        ins.then_inc(rope_step, 1) if half == 0 else ins.then_inc(qk_taken, 1)
                if live2:
                    dve.wait_ge(exp_ready, t2 + 1)
                    if past2(1):
                        dve.wait_ge(norm_step, NORM * t2)
                    dve.tensor_reduce(zsum[:], probs[:, b2].rearrange("p (h g) -> p h g", h=H), AX.X,
                                      ALU.add).then_inc(norm_step, 1)
                if live:
                    dve.wait_ge(qk_taken, t + 1)
                    if past(2):
                        dve.wait_ge(sprod_pool, t - 1)
                        dve.wait_ge(sprod_dve, t - 1)
                    dve.tensor_tensor(qkr[:, b], qk_cos[:], qk_sin[:], ALU.add).then_inc(rope_step, 1)
                if routed:
                    dve.wait_ge(gexp_ready, q + 1)
                    dve.tensor_reduce(gz[:], gexp[:], AX.X, ALU.add).then_inc(route_step, 1)
                if live2:
                    dve.wait_ge(norm_step, NORM * t2 + 1)
                    dve.reciprocal(zinv[:], zsum[:]).then_inc(norm_step, 1)
                if routed:
                    dve.wait_ge(route_step, at + 3)
                    dve.reciprocal(gzinv[:], gz[:]).then_inc(route_step, 1)
                if live:
                    dve.wait_ge(rope_step, ROPE * (t + 1))
                    if past(2):
                        dve.wait_ge(scores_ready, t - 1)
                    qr = qkr[:, b, 0:D].rearrange("p (h o d) -> p d h o", h=H, o=1)[:, 0:dims].broadcast_to([P, dims, H, H])
                    kr = qkr[:, b, D:2 * D].rearrange("p (o g d) -> p d o g", o=1, g=H)[:, 0:dims].broadcast_to([P, dims, H, H])
                    dve.tensor_tensor(sprod[:, b, 0:dims].rearrange("p d (h g) -> p d h g", h=H), qr, kr,
                                      ALU.mult).then_inc(sprod_dve, 1)
                if routed:
                    dve.wait_ge(route_step, at + 4)
                    dve.tensor_tensor(score[:], gexp[:], gzinv[:].rearrange("p (t o) -> p t o", o=1).broadcast_to([P, GT, E]),
                                      ALU.mult).then_inc(route_step, 1)
                if live2:
                    dve.wait_ge(v_copied, t2 + 1)
                    dve.tensor_tensor(
                        vprod[:, 0:heads * DH].rearrange("p (h d) g -> p h d g", h=heads),
                        probs[:, b2, 0:heads * H].rearrange("p (h o g) -> p h o g", h=heads, o=1).broadcast_to([P, heads, DH, H]),
                        v[:, jt2 % GT].rearrange("p (o g d) -> p o d g", o=1, g=H).broadcast_to([P, heads, DH, H]),
                        ALU.mult).then_inc(vprod_dve, 1)
                if routed:
                    dve.wait_ge(route_step, at + 5)
                    after_waits(dve)
                    for n in range(GT):
                        dve.max(top[:, n], score[:, n]).then_inc(route_step, 1)
                if live3:
                    dve.wait_ge(y_ready, t3 + 1)
                    dve.wait_ge(x_in[jt3 % GT], 16 * rounds(m, j, 3))
                    if past3(2):
                        dve.wait_ge(x1_ready, t3 - 1)
                    if past3(1):
                        dve.wait_ge(ln_step, LN * t3)
                    dve.tensor_tensor(res[:, b3], ps_y[:, 0:D], xtok[:, jt3 % GT], ALU.add).then_inc(ln_step, 1)
                if routed:
                    dve.wait_ge(route_step, at + 9)
                    after_waits(dve)
                    for n in range(GT):
                        dve.max_index(topi[:, n], top[:, n], score[:, n]).then_inc(route_step, 1)
                if live1:
                    dve.wait_ge(scores_copied, t1 + 1)
                    if past1(1):
                        dve.wait_ge(diff_ready, t1)
                    dve.tensor_reduce(smax[:], sdiff[:, b1].rearrange("p (h g) -> p h g", h=H), AX.X,
                                      ALU.max).then_inc(max_ready, 1)
                if routed:
                    dve.wait_ge(route_step, at + 13)
                    dve.tensor_copy(topf[:], topi[:, :, 0:TOPK]).then_inc(route_step, 1)
                    dve.scalar_tensor_tensor(out=vsum[:], in0=top[:, :, 0], scalar=GATE_EPS, in1=top[:, :, 1],
                                             op0=ALU.add, op1=ALU.add).then_inc(route_step, 1)
                if live3:
                    dve.wait_ge(ln_step, LN * t3 + 1)
                    dve.bn_stats(stats[:], res[:, b3]).then_inc(ln_step, 1)
                if routed:
                    dve.wait_ge(route_step, at + 14)
                    for s in range(TOPK):
                        dve.tensor_tensor(onehot[:, :, s], iota8[:].rearrange("p (o e) -> p o e", o=1).broadcast_to([P, GT, E]),
                                          topf[:, :, s:s + 1].broadcast_to([P, GT, E]), ALU.is_equal).then_inc(route_step, 1)
                    dve.wait_ge(route_step, at + 15)
                    dve.reciprocal(vinv[:], vsum[:]).then_inc(route_step, 1)
                    dve.wait_ge(route_step, at + 17)
                    dve.tensor_tensor(member[:], onehot[:, :, 0], onehot[:, :, 1], ALU.add).then_inc(route_step, 1)
                    dve.wait_ge(route_step, at + 18)
                    dve.tensor_tensor(comb[:, bass.ds(q * GT, GT)], top[:, :, 0:TOPK],
                                      vinv[:].rearrange("p (t o) -> p t o", o=1).broadcast_to([P, GT, TOPK]),
                                      ALU.mult).then_inc(route_step, 1)
                if routed:
                    dve.wait_ge(count_ready, q + 1)
                    run_b = run[:].rearrange("p (o e) -> p o e", o=1).broadcast_to([P, GT, E])
                    dve.tensor_tensor(pos8[:], ps_pos, run_b, ALU.add).then_inc(route_step, 1)
                if routed:
                    dve.wait_ge(route_step, at + 21)
                    for s in range(TOPK):
                        ins = dve.tensor_tensor(pos_sel[:, :, s], onehot[:, :, s], pos8[:], ALU.mult)
                    ins.then_inc(route_step, 1)
                    dve.tensor_tensor(run[:], run[:], ps_tot, ALU.add).then_inc(route_step, 1)
                    dve.wait_ge(route_step, at + 22)
                    dve.tensor_reduce(posf[:], pos_sel[:], AX.X, ALU.add).then_inc(route_step, 1)
                    dve.wait_ge(route_step, at + 24)
                    dve.tensor_copy(posi[:, k], posf[:]).then_inc(route_step, 1)
                    dve.tensor_copy(pos_x[:, bass.ds(q * GT, GT)], posf[:])
                    dve.tensor_copy(choice[:, bass.ds(q * GT, GT)], topf[:]).then_inc(pos_kept, 1)
                if live2:
                    dve.wait_ge(vprod_pool, t2 + 1)
                    dve.wait_ge(vprod_dve, t2 + 1)
                    dve.tensor_reduce(osum[:], vprod[:], AX.X, ALU.add).then_inc(norm_step, 1)
                if live3:
                    dve.wait_ge(ln_step, LN * t3 + 2)
                    if past3(2):
                        dve.wait_ge(rstd_ready, t3 - 1)
                    after_waits(dve)
                    dve.bn_aggr(mv[:, b3], stats[:]).then_inc(ln_step, 1)
                if live2:
                    dve.wait_ge(norm_step, NORM * t2 + 3)
                    if past2(2):
                        dve.wait_ge(ot_ready, t2 - 1)
                    dve.tensor_tensor(
                        onorm[:, b2].rearrange("p (h d) -> p h d", h=H), osum[:].rearrange("p (h d) -> p h d", h=H),
                        zinv[:].rearrange("p (h o) -> p h o", o=1).broadcast_to([P, H, DH]), ALU.mult).then_inc(norm_step, 1)
                if live3:
                    dve.wait_ge(ln_step, LN * t3 + 3)
                    dve.tensor_scalar(veps[:, b3:b3 + 1], mv[:, b3, 1:2], LN_EPS, None, ALU.add).then_inc(ln_step, 1)

            slots(dve, slot)
            dve.wait_ge(w2_in, 16 * LATE_LOADS)
            dve.wait_ge(pos_kept, NG)
            step = 0

            def table(ins, then=True):
                nonlocal step
                step += 1
                ins.then_inc(table_step, 1)
                if then:
                    dve.wait_ge(table_step, step)

            def over_blocks(a):
                return a.rearrange("p (o e) -> p o e", o=1).broadcast_to([P, NB, E])

            def over_experts(a):
                return a.rearrange("p (b o) -> p b o", o=1).broadcast_to([P, NB, E])

            table(dve.tensor_copy(tab_end[:], run[:]), then=False)
            table(dve.tensor_tensor(count[:], run[:], base8[:], ALU.subtract))
            table(dve.tensor_scalar(count_i[:], count[:], float(BR - 1), None, ALU.add))
            table(dve.tensor_scalar(blocks_i[:], count_i[:], BR.bit_length() - 1, None, ALU.logical_shift_right))
            table(dve.tensor_copy(blocks[:], blocks_i[:]))
            table(dve.tensor_tensor_scan(blocks_to[:], ones[:, 0:E], blocks[:], 0.0, ALU.mult, ALU.add))
            table(dve.tensor_tensor(passed, over_experts(iotab[:]), over_blocks(blocks_to[:]), ALU.is_ge))
            table(dve.tensor_reduce(expert_raw[:], passed, AX.X, ALU.add))
            table(dve.tensor_scalar(expert[:], expert_raw[:], float(E - 1), None, ALU.min))
            table(dve.tensor_tensor(is_expert, over_blocks(iota8[:]), over_experts(expert[:]), ALU.is_equal))
            table(dve.tensor_tensor(first_row[:], blocks_to[:], blocks[:], ALU.subtract))
            table(dve.scalar_tensor_tensor(out=first_row[:], in0=first_row[:], scalar=-float(BR), in1=base8[:],
                                           op0=ALU.mult, op1=ALU.add))
            table(dve.tensor_tensor(passed, is_expert, over_blocks(first_row[:]), ALU.mult))
            table(dve.tensor_reduce(row[:], passed, AX.X, ALU.add))
            table(dve.scalar_tensor_tensor(out=row[:], in0=iotab[:], scalar=float(BR), in1=row[:], op0=ALU.mult, op1=ALU.add))
            table(dve.tensor_scalar(unused[:], expert_raw[:], float(E) - 0.5, None, ALU.is_ge))
            table(dve.tensor_scalar(row_fix[:], row[:], -1.0, float(ZROW), ALU.mult, ALU.add))
            table(dve.tensor_tensor(row_fix[:], row_fix[:], unused[:], ALU.mult))
            table(dve.tensor_tensor(tab_row[:], row[:], row_fix[:], ALU.add), then=False)
            table(dve.tensor_copy(tab_expert[:], expert[:]))
            choices = choice[:].rearrange("p t (s o) -> p (t s) o", o=1).broadcast_to([P, T * TOPK, E])
            table(dve.tensor_tensor(of_expert, iota8[:].rearrange("p (o e) -> p o e", o=1)
                                    .broadcast_to([P, T * TOPK, E]), choices, ALU.is_equal))
            table(dve.tensor_tensor(of_expert, of_expert, first_row[:].rearrange("p (o e) -> p o e", o=1)
                                    .broadcast_to([P, T * TOPK, E]), ALU.mult))
            table(dve.tensor_reduce(shift[:], of_expert, AX.X, ALU.add))
            table(dve.tensor_tensor(pos[:].rearrange("p t s -> p (t s)"), pos_x[:].rearrange("p t s -> p (t s)"),
                                    shift[:], ALU.subtract), then=False)
            assert step == TABLE
            dve.wait_ge(wo_hi_done, 1)
            dve.tensor_tensor(wo_lo[:], wo_raw[:], wo_hi[:], ALU.subtract).then_inc(wo_lo_done, 1)

            def block_slot(m, j, steady):
                b, jb, live, past = block_of(m, j, 2, steady)
                if live:
                    e = dve.value_load(tab_expert[0:1, bass.ds(b, 1)], min_val=0, max_val=E - 1)
                    if past(3):
                        dve.wait_ge(yrow_ready, b - 2)
                    for c in range(CH):
                        dve.wait_ge(sig_ready, CH * b + c + 1)
                        if past(1):
                            dve.wait_ge(g_step, GATED * (b - 1) + 3 * (c + 1))
                        dve.scalar_tensor_tensor(
                            out=gated[:, c], in0=hidden_bank[c][:, 0:BR],
                            scalar=b1[:, bass.ds(e, 1), 0, c:c + 1].rearrange("p o n -> p (o n)"),
                            in1=sig[:, c], op0=ALU.add, op1=ALU.mult).then_inc(g_step, 1)
                        dve.wait_ge(g_step, GATED * b + 3 * c + 1)
                        dve.tensor_copy(g_hi[:, jb, c], gated[:, c]).then_inc(g_step, 1)
                        dve.wait_ge(g_step, GATED * b + 3 * c + 2)
                        dve.tensor_tensor(g_lo[:, jb, c], gated[:, c], g_hi[:, jb, c], ALU.subtract).then_inc(g_step, 1)

            block_slots(dve, block_slot)

            def group_slot(m, j, steady):
                g, k, live, past = late_group(m, j, 0, steady)
                if live:
                    for step in range(GT + 3):
                        n = step
                        if n < GT:
                            dve.wait_ge(xr_in[k][n], 16 * (m + 1))
                            dve.wait_ge(gathered[k][n], 32 * (m + 1))
                            if past(2) and n == 0:
                                dve.wait_ge(out_ready, g - 1)
                            dve.scalar_tensor_tensor(out=res3[:, k, n], in0=yg[:, k, n, 0], scalar=comb[:, bass.ds(g * GT + n, 1), 0],
                                                     in1=xr[:, k, n], op0=ALU.mult, op1=ALU.add).then_inc(mixed_first, 1)
                        n = step - 1
                        if 0 <= n < GT:
                            dve.wait_ge(mixed_first, GT * g + n + 1)
                            dve.scalar_tensor_tensor(out=res3[:, k, n], in0=yg[:, k, n, 1], scalar=comb[:, bass.ds(g * GT + n, 1), 1],
                                                     in1=res3[:, k, n], op0=ALU.mult, op1=ALU.add).then_inc(mixed, 1)
                        n = step - 2
                        if 0 <= n < GT:
                            dve.wait_ge(mixed, GT * g + n + 1)
                            if past(1):
                                dve.wait_ge(mv_ready, GT * (g - 1) + n + 1)
                            dve.bn_stats(stats3[:, n], res3[:, k, n]).then_inc(stats_ready, 1)
                        n = step - 3
                        if 0 <= n < GT:
                            dve.wait_ge(stats_ready, GT * g + n + 1)
                            after_waits(dve)
                            dve.bn_aggr(mv3[:, k, n], stats3[:, n]).then_inc(mv_ready, 1)
                    dve.wait_ge(mv_ready, GT * (g + 1))
                    if past(1):
                        dve.wait_ge(rstd3_ready, g)
                    dve.tensor_scalar(veps3[:], mv3[:, k, :, 1], LN_EPS, None, ALU.add).then_inc(veps3_ready, 1)
                g, k, live, past = late_group(m, j, 1, steady)
                if live:
                    dve.wait_ge(rstd3_ready, g + 1)
                    if past(2):
                        dve.wait_ge(stored[k], 16 * (m + (j - 1) // 2))
                    for n in range(GT):
                        ins = dve.tensor_scalar(o3[:, k, n], res3[:, k, n], mv3[:, k, n, 0:1], rstd3[:, k, n:n + 1],
                                                ALU.subtract, ALU.mult)
                    ins.then_inc(out_ready, 1)

            group_slots(dve, group_slot)


_CONSTANTS = ("rope", "eye", "before", "ones", "iota8", "base8")


def arrange(inputs):
    g = {k.split("_", 1)[1]: np.asarray(v) for k, v in inputs.items()}
    x = g["attn_x"].reshape(T, P, D)
    wup = g["attn_Wup"].reshape(LAT, H, 2, DH).transpose(0, 2, 1, 3).reshape(LAT, 2 * D)
    bup = g["attn_bup"].reshape(H, 2, DH).transpose(1, 0, 2).reshape(2 * D)

    def rows(a, n):
        return np.broadcast_to(a, (P, n))

    def chunks(a):
        return a.reshape(NC, P, -1).transpose(1, 0, 2)

    d = {
        "x": x,
        "xT": x.reshape(T, P, NC, P).transpose(0, 3, 2, 1),
        "wq": chunks(g["attn_Wq"]),
        "wdown": chunks(g["attn_Wdown"]),
        "bdown": g["attn_bdown"].reshape(LAT, 1),
        "wup": np.concatenate([wup, bup.reshape(1, 2 * D)], 0),
        "bq": g["attn_bq"].reshape(1, D),
        "wout": chunks(g["attn_Wout"]),
        "bout": g["attn_bout"].reshape(1, D),
        "wg": chunks(g["ffn_Wg"].T),
        "w1": g["ffn_W1"].transpose(0, 2, 1).reshape(E, NC, P, 2 * HID).transpose(0, 2, 1, 3).reshape(E, P, NC * 2 * HID),
        "b1": g["ffn_b1"].reshape(E, 2, HID // P, P).transpose(3, 0, 1, 2),
        "wo": g["ffn_Wo"].T.reshape(HID // P, P, D).transpose(1, 0, 2),
        "bo": rows(g["ffn_bo"], D),
    }
    d.update(shape_constants())
    return {k: np.ascontiguousarray(v) for k, v in d.items()}


def kernel(**inputs):
    import concourse.bacc as _bacc
    from concourse.bass_utils import run_bass_kernel_spmd as _run

    nc = _bacc.Bacc("TRN2", target_bir_lowering=False, num_devices=1)
    arrays, args = {}, {}
    for name, a in arrange(inputs).items():
        arrays[f"in_{name}_dram"] = a
        args[name] = nc.dram_tensor(f"in_{name}_dram", a.shape, mybir.dt.from_np(a.dtype), kind="ExternalInput").ap()
    out = nc.dram_tensor("out_0_dram", (N, D), F32, kind="ExternalOutput").ap()
    postln_kernel(nc, args, out)
    r = _run(nc, [arrays], core_ids=[0])
    return r.results[0]["out_0_dram"].reshape(4, 1024, D)
```
